# Optimizing a Trainium2 kernel written in Bass

```python
import numpy as np
import jax
import jax.numpy as jnp

def _softmax(x, axis=-1):
    return jax.nn.softmax(x, axis=axis)

def _gelu(x):
    return jax.nn.gelu(x, approximate=True)

def _silu(x):
    return jax.nn.silu(x)

def _sigmoid(x):
    return jax.nn.sigmoid(x)

def _layernorm(x, axis=-1, eps=1e-05):
    m = jnp.mean(x, axis=axis, keepdims=True)
    v = jnp.var(x, axis=axis, keepdims=True)
    return (x - m) / jnp.sqrt(v + eps)

def _scatter_add(tgt, idx, src, axis=0):
    return tgt.at[idx].add(src)

def _segment_sum(src, seg, n):
    return jax.ops.segment_sum(src, seg, n)
kernel_name = 'mk_prb_d1_jaxref_r8_3a9162'

def setup_inputs(seed: int=0):
    np.random.seed(seed)
    _w = jnp.asarray

    def _L0_attn_setup():
        import jax, jax.numpy as jnp
        import numpy as np
        import math
        B_SZ, T_LEN = (2, 128)
        D_MODEL, D_STATE, D_CONV, EXPAND = (128, 16, 4, 2)
        D_INNER = EXPAND * D_MODEL
        DT_RANK = math.ceil(D_MODEL / 16)

        def _mamba_forward(x, norm_w, in_proj_w, conv_w, conv_b, x_proj_w, dt_proj_w, dt_proj_b, A_log, D_param, out_proj_w):
            residual = x
            eps = jnp.finfo(x.dtype).eps
            xn = x * jax.lax.rsqrt(jnp.mean(x * x, axis=-1, keepdims=True) + eps) * norm_w
            xz = xn @ in_proj_w.T
            x_s, z = (xz[..., :D_INNER], xz[..., D_INNER:])
            u = jax.lax.conv_general_dilated(x_s.transpose(0, 2, 1), conv_w, window_strides=(1,), padding=[(D_CONV - 1, 0)], dimension_numbers=('NCH', 'OIH', 'NCH'), feature_group_count=D_INNER) + conv_b[None, :, None]
            u = jax.nn.silu(u).transpose(0, 2, 1)
            x_dbc = u @ x_proj_w.T
            dt_raw = x_dbc[..., :DT_RANK]
            B_ssm = x_dbc[..., DT_RANK:DT_RANK + D_STATE]
            C_ssm = x_dbc[..., DT_RANK + D_STATE:]
            delta = jax.nn.softplus(dt_raw @ dt_proj_w.T + dt_proj_b)
            A = -jnp.exp(A_log)
            dA = jnp.exp(jnp.einsum('bti,is->btis', delta, A))
            dBu = jnp.einsum('bti,bts->btis', delta * u, B_ssm)

            def step(h, inp):
                dA_t, dBu_t, C_t = inp
                h = dA_t * h + dBu_t
                y_t = jnp.einsum('bis,bs->bi', h, C_t)
                return (h, y_t)
            h0 = jnp.zeros((x.shape[0], D_INNER, D_STATE), x.dtype)
            _, ys = jax.lax.scan(step, h0, (dA.transpose(1, 0, 2, 3), dBu.transpose(1, 0, 2, 3), C_ssm.transpose(1, 0, 2)))
            y = ys.transpose(1, 0, 2) + u * D_param
            y = y * jax.nn.silu(z)
            return y @ out_proj_w.T + residual
        key = jax.random.key(seed)
        ks = jax.random.split(key, 10)
        f32 = jnp.float32
        x = jax.random.normal(ks[0], (B_SZ, T_LEN, D_MODEL), f32)
        norm_w = jnp.ones((D_MODEL,), f32)
        in_proj_w = jax.random.normal(ks[1], (2 * D_INNER, D_MODEL), f32) / np.sqrt(D_MODEL)
        conv_w = jax.random.uniform(ks[2], (D_INNER, 1, D_CONV), f32, -0.5, 0.5)
        conv_b = jax.random.uniform(ks[3], (D_INNER,), f32, -0.5, 0.5)
        x_proj_w = jax.random.normal(ks[4], (DT_RANK + 2 * D_STATE, D_INNER), f32) / np.sqrt(D_INNER)
        dt_std = DT_RANK ** (-0.5)
        dt_proj_w = jax.random.uniform(ks[5], (D_INNER, DT_RANK), f32, -dt_std, dt_std)
        dt = jnp.exp(jax.random.uniform(ks[6], (D_INNER,), f32) * (np.log(0.1) - np.log(0.001)) + np.log(0.001))
        dt_proj_b = dt + jnp.log(-jnp.expm1(-dt))
        A_log = jnp.log(jnp.tile(jnp.arange(1, D_STATE + 1, dtype=f32)[None, :], (D_INNER, 1)))
        D_param = jnp.ones((D_INNER,), f32)
        out_proj_w = jax.random.normal(ks[7], (D_MODEL, D_INNER), f32) / np.sqrt(D_INNER)
        return {'x': x, 'norm_w': norm_w, 'in_proj_w': in_proj_w, 'conv_w': conv_w, 'conv_b': conv_b, 'x_proj_w': x_proj_w, 'dt_proj_w': dt_proj_w, 'dt_proj_b': dt_proj_b, 'A_log': A_log, 'D_param': D_param, 'out_proj_w': out_proj_w}
    _L0_attn_in = _L0_attn_setup()

    def _L0_ffn_setup():
        import jax, jax.numpy as jnp
        import numpy as np
        NUM_EXPERTS = 8
        TOP_K = 2
        HIDDEN = 128
        INTER = 352
        key = jax.random.key(seed)
        ks = jax.random.split(key, 5)
        scale = 0.02
        return {'x': jax.random.normal(ks[0], (4, 256, HIDDEN), dtype=jnp.float32), 'w_router': jax.random.normal(ks[1], (NUM_EXPERTS, HIDDEN), dtype=jnp.float32) * scale, 'w_gate': jax.random.normal(ks[2], (NUM_EXPERTS, HIDDEN, INTER), dtype=jnp.float32) * scale, 'w_up': jax.random.normal(ks[3], (NUM_EXPERTS, HIDDEN, INTER), dtype=jnp.float32) * scale, 'w_down': jax.random.normal(ks[4], (NUM_EXPERTS, INTER, HIDDEN), dtype=jnp.float32) * scale}
    _L0_ffn_in = _L0_ffn_setup()
    _d = {'L0_attn_x': _L0_attn_in['x'], 'L0_attn_norm_w': _L0_attn_in['norm_w'], 'L0_attn_in_proj_w': _L0_attn_in['in_proj_w'], 'L0_attn_conv_w': _L0_attn_in['conv_w'], 'L0_attn_conv_b': _L0_attn_in['conv_b'], 'L0_attn_x_proj_w': _L0_attn_in['x_proj_w'], 'L0_attn_dt_proj_w': _L0_attn_in['dt_proj_w'], 'L0_attn_dt_proj_b': _L0_attn_in['dt_proj_b'], 'L0_attn_A_log': _L0_attn_in['A_log'], 'L0_attn_D_param': _L0_attn_in['D_param'], 'L0_attn_out_proj_w': _L0_attn_in['out_proj_w'], 'L0_ffn_w_router': _L0_ffn_in['w_router'], 'L0_ffn_w_gate': _L0_ffn_in['w_gate'], 'L0_ffn_w_up': _L0_ffn_in['w_up'], 'L0_ffn_w_down': _L0_ffn_in['w_down']}
    _x0 = _d['L0_attn_x']
    _d['L0_attn_x'] = jax.random.normal(jax.random.fold_in(jax.random.key(seed), 1), (8, 512, 128), dtype=_x0.dtype)
    del _x0
    return _d

def reference(L0_attn_x, L0_attn_norm_w, L0_attn_in_proj_w, L0_attn_conv_w, L0_attn_conv_b, L0_attn_x_proj_w, L0_attn_dt_proj_w, L0_attn_dt_proj_b, L0_attn_A_log, L0_attn_D_param, L0_attn_out_proj_w, L0_ffn_w_router, L0_ffn_w_gate, L0_ffn_w_up, L0_ffn_w_down):

    def _L0_attn_ref(x, norm_w, in_proj_w, conv_w, conv_b, x_proj_w, dt_proj_w, dt_proj_b, A_log, D_param, out_proj_w):
        import jax, jax.numpy as jnp
        import numpy as np
        import math
        B_SZ, T_LEN = (2, 128)
        D_MODEL, D_STATE, D_CONV, EXPAND = (128, 16, 4, 2)
        D_INNER = EXPAND * D_MODEL
        DT_RANK = math.ceil(D_MODEL / 16)

        def _mamba_forward(x, norm_w, in_proj_w, conv_w, conv_b, x_proj_w, dt_proj_w, dt_proj_b, A_log, D_param, out_proj_w):
            residual = x
            eps = jnp.finfo(x.dtype).eps
            xn = x * jax.lax.rsqrt(jnp.mean(x * x, axis=-1, keepdims=True) + eps) * norm_w
            xz = xn @ in_proj_w.T
            x_s, z = (xz[..., :D_INNER], xz[..., D_INNER:])
            u = jax.lax.conv_general_dilated(x_s.transpose(0, 2, 1), conv_w, window_strides=(1,), padding=[(D_CONV - 1, 0)], dimension_numbers=('NCH', 'OIH', 'NCH'), feature_group_count=D_INNER) + conv_b[None, :, None]
            u = jax.nn.silu(u).transpose(0, 2, 1)
            x_dbc = u @ x_proj_w.T
            dt_raw = x_dbc[..., :DT_RANK]
            B_ssm = x_dbc[..., DT_RANK:DT_RANK + D_STATE]
            C_ssm = x_dbc[..., DT_RANK + D_STATE:]
            delta = jax.nn.softplus(dt_raw @ dt_proj_w.T + dt_proj_b)
            A = -jnp.exp(A_log)
            dA = jnp.exp(jnp.einsum('bti,is->btis', delta, A))
            dBu = jnp.einsum('bti,bts->btis', delta * u, B_ssm)

            def step(h, inp):
                dA_t, dBu_t, C_t = inp
                h = dA_t * h + dBu_t
                y_t = jnp.einsum('bis,bs->bi', h, C_t)
                return (h, y_t)
            h0 = jnp.zeros((x.shape[0], D_INNER, D_STATE), x.dtype)
            _, ys = jax.lax.scan(step, h0, (dA.transpose(1, 0, 2, 3), dBu.transpose(1, 0, 2, 3), C_ssm.transpose(1, 0, 2)))
            y = ys.transpose(1, 0, 2) + u * D_param
            y = y * jax.nn.silu(z)
            return y @ out_proj_w.T + residual
        return _mamba_forward(x, norm_w, in_proj_w, conv_w, conv_b, x_proj_w, dt_proj_w, dt_proj_b, A_log, D_param, out_proj_w)

    def _L0_ffn_ref(x, w_router, w_gate, w_up, w_down):
        import jax, jax.numpy as jnp
        import numpy as np
        NUM_EXPERTS = 8
        TOP_K = 2
        HIDDEN = 128
        INTER = 352
        B, S, H = x.shape
        T = B * S
        E = w_router.shape[0]
        xf = x.reshape(T, H)
        logits = xf @ w_router.T
        top_w, sel = jax.lax.top_k(logits, TOP_K)
        top_w = jax.nn.softmax(top_w, axis=-1)
        gates = jnp.zeros((T, E), dtype=x.dtype).at[jnp.arange(T)[:, None], sel].add(top_w)
        out = jnp.zeros_like(xf)
        for e in range(E):
            h = jax.nn.silu(xf @ w_gate[e]) * (xf @ w_up[e])
            out = out + gates[:, e:e + 1] * (h @ w_down[e])
        return out.reshape(B, S, H)
    x = L0_attn_x
    xn = _layernorm(x, axis=-1)
    x = x + _L0_attn_ref(xn, L0_attn_norm_w, L0_attn_in_proj_w, L0_attn_conv_w, L0_attn_conv_b, L0_attn_x_proj_w, L0_attn_dt_proj_w, L0_attn_dt_proj_b, L0_attn_A_log, L0_attn_D_param, L0_attn_out_proj_w) + _L0_ffn_ref(xn, L0_ffn_w_router, L0_ffn_w_gate, L0_ffn_w_up, L0_ffn_w_down)
    return x

_drawn_inputs = setup_inputs


def setup_inputs(seed=0):
    import zlib

    import numpy as np

    out = dict(_drawn_inputs(seed))
    spreads = {'L0_attn_norm_w': (1.0, 0.2), 'L0_attn_D_param': (1.0, 0.566)}
    factors = {'L0_attn_x_proj_w': 7.63,
     'L0_attn_dt_proj_w': 8.0,
     'L0_attn_dt_proj_b': 8.0,
     'L0_attn_A_log': 8.0,
     'L0_ffn_w_router': 8.0,
     'L0_ffn_w_gate': 8.0,
     'L0_ffn_w_up': 8.0,
     'L0_ffn_w_down': 8.0}
    for name, (base, spread) in spreads.items():
        noise = np.random.default_rng([zlib.crc32(name.encode()), seed]).standard_normal(out[name].shape)
        drawn = base * np.exp(spread * noise) if base else spread * noise
        out[name] = jnp.asarray(drawn.astype(out[name].dtype))
    for name, factor in factors.items():
        out[name] = (out[name] * factor).astype(out[name].dtype)
    return out
```

```python
import numpy as np
import concourse.bass as bass
from concourse import mybir
from contextlib import ExitStack

FP32 = mybir.dt.float32
ALU = mybir.AluOpType
ACT = mybir.ActivationFunctionType
AX = mybir.AxisListType


def build(nc, x, norm_w, w_in, conv_w, conv_b, x_proj, dt_proj, dt_b, a_log, d_par, w_out,
          w_router, w_gate, w_up, w_down, ident, rank8, out):
    P = 128
    NB, T, H = 8, 512, 128
    TT = T // P
    NT = NB * TT
    NH = 2
    C = NH * P
    S = 16
    K = conv_w.shape[0]
    R = dt_proj.shape[0]
    E, F = w_gate.shape[0], w_gate.shape[2]
    FC = [(0, 128), (128, 128), (256, F - 256)]
    LN_EPS = 1e-5
    RMS_EPS = float(np.finfo(np.float32).eps)
    ST_LN, ST_RMS, ST_NORM, ST_TOP = 7, 15, 20, 33

    ctx = ExitStack()
    with ctx:
        def sb(name, shape, dt=FP32):
            return ctx.enter_context(nc.sbuf_tensor(name, shape, dt))

        def sem(name):
            return ctx.enter_context(nc.semaphore(name))

        id_sb = sb("id_sb", [P, P])
        rank_sb = sb("rank_sb", [P, E])
        nw_sb = sb("nw_sb", [P, 1])
        win_sb = sb("win_sb", [P, NH * C])
        cw_sb = sb("cw_sb", [P, K, C])
        wk_sb = sb("wk_sb", [P, K, C])
        wz_sb = sb("wz_sb", [P, C])
        cb_sb = sb("cb_sb", [P, NH])
        xp_sb = sb("xp_sb", [P, NH, R + 2 * S])
        dtw_sb = sb("dtw_sb", [R, C])
        dtb_sb = sb("dtb_sb", [P, NH])
        a_sb = sb("a_sb", [P, NH, S])
        d_sb = sb("d_sb", [P, NH])
        wo_sb = sb("wo_sb", [P, NH, H])
        wr_sb = sb("wr_sb", [P, E])
        wg_sb = sb("wg_sb", [P, E, F])
        wu_sb = sb("wu_sb", [P, E, F])
        wd_sb = sb("wd_sb", [P, E, 3, H])

        x_sb = sb("x_sb", [P, NT, H])
        stat = sb("stat", [P, NT, 6])
        tmp = [sb(f"tmp{i}", [P, NT]) for i in range(4)]
        mean = sb("mean", [P, NT])
        rstd = sb("rstd", [P, NT])
        rms = sb("rms", [P, NT])
        xn_st = sb("xn_st", [P, TT, H])
        xh_st = sb("xh_st", [P, TT, H])
        xnT = sb("xnT", [P, NB * T])
        xhT = sb("xhT", [P, NB, T + K - 1])
        xnT_st = sb("xnT_st", [P, T])

        lg = sb("lg", [P, NT, E])
        oh1 = sb("oh1", [P, NT, E])
        oh2 = sb("oh2", [P, NT, E])
        key = sb("key", [P, NT, E])
        m1 = sb("m1", [P, NT])
        m2 = sb("m2", [P, NT])
        kk = sb("kk", [P, NT])
        p1 = sb("p1", [P, NT])
        p2 = sb("p2", [P, NT])
        gates = sb("gates", [P, NT, E])

        acc = x_sb
        sg = sb("sg", [P, 3, T])
        hT = sb("hT", [P, 3, T])

        u_sb = [sb(f"u_sb{i}", [P, NH, T]) for i in range(2)]
        zs_sb = [sb(f"zs_sb{i}", [P, NH, T]) for i in range(2)]
        delta = [sb(f"delta{i}", [P, NH, T]) for i in range(2)]
        duT = [sb(f"duT{i}", [P, TT, C]) for i in range(2)]
        bc_sb = [sb(f"bc_sb{i}", [P, TT, 2 * S]) for i in range(2)]
        dtr_sb = sb("dtr_sb", [R, T])
        sp_m = sb("sp_m", [P, NH, T])
        sp_a = sb("sp_a", [P, NH, T])
        sp_y = sb("sp_y", [P, NH, T])
        sp_l = sb("sp_l", [P, NH, T])
        sp_d = sb("sp_d", [P, NH, T])
        du = sb("du", [P, NH, T])
        dbuT = [sb(f"dbuT{i}", [P, TT, C]) for i in range(2)]
        parts = [xnT[:, i * NH * T:(i + 1) * NH * T].rearrange("p (a c) -> p a c", a=NH) for i in range(4)]
        da, h_sb = parts[0:2], parts[2:4]
        y_sb = sb("y_sb", [P, TT, C])
        g_sb = sb("g_sb", [P, NH, T])

        bank = [ctx.enter_context(nc.psum_tensor(f"bank{i}", [P, 512], FP32)) for i in range(8)]
        DBU = bank[0:2]
        HT = [bank[2 + q][:, :].rearrange("p (a c) -> p a c", a=2) for q in range(2)]
        FB = bank[4:6]

        names = """in_small in_taps in_x in_moe w_scaled a_ready stats_bn st rms_rt xn_w xh_w xn_pe xnT_a xnT_c xh_pe xhT_c
                   lgmm lg_c rt exp_rt rt_p x_pad acc_w g_mm u_mm sg_rdy ht_w y_mm ep_acc gates_rdy
                   dbuT_rdy dbu_rdy da_rdy h_rdy ht_rdy y_acc
                   xc_mm u_rdy dtr_mm dtr_rdy v_mm v_out bc_mm bc_rdy z_mm z_rdy sp_exp sp_ln
                   sp_pool delta_rdy du_rdy dut_mm dut_rdy yb_mm g_sum g_rdy o_mm o_rdy o_out pool_go""".split()
        s = {k: sem(k) for k in names}

        def wait(eng, name, val):
            if isinstance(val, int) and val <= 0:
                return
            eng.wait_ge(s[name], val)

        block = ctx.enter_context(nc.Block())

        x_v = x.rearrange("(n p) h -> p n h", p=P)
        out_v = out.rearrange("(n p) h -> p n h", p=P)
        SMALL = 16 * 12

        @block.sync
        def _(sp):
            for b in range(NB):
                sp.dma_start(x_sb[:, b * TT:(b + 1) * TT, :], x_v[:, b * TT:(b + 1) * TT, :]).then_inc(s["in_x"], 16)
            sp.dma_start(wg_sb[:, :, :], w_gate.rearrange("e h f -> h e f")).then_inc(s["in_moe"], 16)
            sp.dma_start(wu_sb[:, :, :], w_up.rearrange("e h f -> h e f")).then_inc(s["in_moe"], 16)
            for c, (f0, fn) in enumerate(FC):
                sp.dma_start(wd_sb[0:fn, :, c, :], w_down[:, f0:f0 + fn, :].rearrange("e f h -> f e h")).then_inc(s["in_moe"], 16)
            for b in range(NB):
                sp.wait_ge(s["o_rdy"], b + 1)
                sp.dma_start(out_v[:, b * TT:(b + 1) * TT, :], acc[:, b * TT:(b + 1) * TT, :]).then_inc(s["o_out"], 16)
            sp.wait_ge(s["o_out"], 16 * NB)

        @block.scalar
        def _(act):
            for dst, src in ((id_sb[:, :], ident), (rank_sb[:, :], rank8), (nw_sb[:, :], norm_w), (win_sb[:, :], w_in),
                             (cb_sb[:, :], conv_b), (dtb_sb[:, :], dt_b), (d_sb[:, :], d_par), (dtw_sb[:, :], dt_proj),
                             (wr_sb[:, :], w_router), (xp_sb[:, :, :], x_proj), (wo_sb[:, :, :], w_out),
                             (a_sb[:, :, :], a_log)):
                act.dma_start(dst, src).then_inc(s["in_small"], 16)
            act.wait_ge(s["in_small"], SMALL)
            nc.scalar.activation(a_sb[:, :, :], a_sb[:, :, :], ACT.Exp).then_inc(s["a_ready"], 1)
            act.wait_ge(s["st"], ST_LN)
            nc.scalar.activation(tmp[1][:, :], tmp[0][:, :], ACT.Sqrt).then_inc(s["rms_rt"], 1)
            act.wait_ge(s["st"], ST_RMS)
            nc.scalar.activation(tmp[1][:, :], tmp[0][:, :], ACT.Sqrt).then_inc(s["rms_rt"], 1)
            act.wait_ge(s["st"], ST_NORM)

            def rescale(b):
                act.wait_ge(s["xn_w"], b * TT + TT)
                wait(act, "xh_pe", b)
                for t in range(TT):
                    nc.scalar.activation(xh_st[:, t, :], xn_st[:, t, :], ACT.Copy,
                                         scale=rms[:, bass.ds(b * TT + t, 1)]).then_inc(s["xh_w"], 1)
                act.wait_ge(s["xn_pe"], b + 1)
                wait(act, "lgmm", TT * b)
                act.wait_ge(s["xnT_c"], b + 1)
                nc.scalar.activation(xnT_st[:, :], bank[0][:, :], ACT.Copy).then_inc(s["xnT_a"], 1)
                act.wait_ge(s["xh_pe"], b + 1)
                nc.scalar.activation(xhT[:, bass.ds(b, 1), K - 1:], bank[1][:, :], ACT.Copy).then_inc(s["xhT_c"], 1)

            rescale(0)
            with act.Fori(1, NB) as b:
                rescale(b)
            act.wait_ge(s["st"], ST_TOP)
            nc.scalar.activation(p2[:, :], kk[:, :], ACT.Exp).then_inc(s["exp_rt"], 1)

            def gate_silu(b):
                for e in range(E):
                    for c, (f0, fn) in enumerate(FC):
                        m = b * E + e
                        act.wait_ge(s["g_mm"], m * 3 + c + 1)
                        wait(act, "ht_w", 3 * (m - 1) + c + 1)
                        nc.scalar.activation(sg[0:fn, c, :], bank[c][0:fn, :], ACT.Silu).then_inc(s["sg_rdy"], 1)

            gate_silu(0)
            with act.Fori(1, NB) as b:
                gate_silu(b)

            def step(b, q, k, more):
                n = b * S + k
                for hf in range(NH):
                    wait(act, "h_rdy", 2 * (n - 2) + hf + 1)
                    if k == 0 and hf == 0:
                        act.wait_ge(s["delta_rdy"], b + 1)
                    nc.scalar.activation(da[k % 2][:, hf, :], delta[q][:, hf, :], ACT.Exp,
                                         scale=a_sb[:, hf, k:k + 1]).then_inc(s["da_rdy"], 1)
                if more:
                    front(b + 1, 1 - q, k)

            def front(b, q, k):
                if k == 4:
                    wait(act, "g_sum", 2 * (b - 1))
                    wait(act, "du_rdy", b - 1)
                    for hf in range(NH):
                        act.wait_ge(s["xc_mm"], 2 * b + hf + 1)
                        nc.scalar.activation(u_sb[q][:, hf, :], FB[hf][:, :], ACT.Silu,
                                             bias=cb_sb[:, hf:hf + 1]).then_inc(s["u_rdy"], 1)
                    act.wait_ge(s["dtr_mm"], b + 1)
                    nc.scalar.activation(dtr_sb[:, :], FB[0][0:R, :], ACT.Copy).then_inc(s["dtr_rdy"], 1)
                if k == 6:
                    wait(act, "delta_rdy", b)
                    for hf in range(NH):
                        act.wait_ge(s["v_mm"], 2 * b + hf + 1)
                        nc.scalar.activation(sp_m[:, hf, :], FB[1 - hf][:, :], ACT.Relu, bias=dtb_sb[:, hf:hf + 1])
                        nc.scalar.activation(sp_a[:, hf, :], FB[1 - hf][:, :], ACT.Abs,
                                             bias=dtb_sb[:, hf:hf + 1]).then_inc(s["v_out"], 1)
                    act.wait_ge(s["v_out"], 2 * b + 2)
                    nc.scalar.activation(sp_y[:, :, :], sp_a[:, :, :], ACT.Exp, scale=-1.0).then_inc(s["sp_exp"], 1)
                    act.wait_ge(s["sp_exp"], b + 1)
                    nc.scalar.activation(sp_l[:, :, :], sp_y[:, :, :], ACT.Ln, bias=1.0).then_inc(s["sp_ln"], 1)
                if k == 7:
                    act.wait_ge(s["bc_mm"], b + 1)
                    nc.scalar.activation(bc_sb[q][:, :, :], FB[1][:, 0:TT * 2 * S].rearrange("p (t c) -> p t c", t=TT),
                                         ACT.Copy).then_inc(s["bc_rdy"], 1)
                if k == 9:
                    wait(act, "g_rdy", 2 * (b - 1))
                    for hf in range(NH):
                        act.wait_ge(s["z_mm"], 2 * b + hf + 1)
                        nc.scalar.activation(zs_sb[q][:, hf, :], FB[hf][:, :], ACT.Silu).then_inc(s["z_rdy"], 1)
                if k in (13, 14):
                    i = k - 13
                    act.wait_ge(s["dut_mm"], 2 * b + i + 1)
                    nc.scalar.activation(duT[q][:, 2 * i:2 * i + 2, :], FB[1 - i][:, :].rearrange("p (a c) -> p a c", a=2),
                                         ACT.Copy).then_inc(s["dut_rdy"], 1)

            for k in range(S):
                front(0, 0, k)
            act.wait_ge(s["y_mm"], NB * E)
            for k in range(S):
                step(0, 0, k, True)
            with act.Fori(0, (NB - 2) // 2) as j:
                for k in range(S):
                    step(2 * j + 1, 1, k, True)
                for k in range(S):
                    step(2 * j + 2, 0, k, True)
            for k in range(S):
                step(NB - 1, 1, k, False)

        @block.gpsimd
        def _(pool):
            with nc.allow_non_contiguous_dma(reason="taps over all partitions"):
                pool.dma_start(cw_sb[:, :, :].rearrange("p k c -> p (k c)"),
                               conv_w.rearrange("(a k) c -> a (k c)", a=1).to_broadcast([P, K * C])).then_inc(s["in_taps"], 16)
            nc.gpsimd.memset(xhT[:, :, 0:K - 1], 0.0).then_inc(s["x_pad"], 1)
            pool.wait_ge(s["in_small"], SMALL)
            pool.wait_ge(s["in_taps"], 16)
            pool.wait_ge(s["a_ready"], 1)
            nc.gpsimd.tensor_scalar(a_sb[:, :, :], a_sb[:, :, :], -1.0, 1.0, ALU.mult, ALU.mult).then_inc(s["w_scaled"], 1)
            nc.gpsimd.tensor_scalar(wz_sb[:, :], win_sb[:, C:2 * C], nw_sb[:, 0:1], 1.0, ALU.mult, ALU.mult).then_inc(s["w_scaled"], 1)
            nc.gpsimd.tensor_scalar(wk_sb[:, 0, :], win_sb[:, 0:C], nw_sb[:, 0:1], 1.0, ALU.mult, ALU.mult).then_inc(s["w_scaled"], 1)
            pool.wait_ge(s["w_scaled"], 3)
            for k in range(K - 1, -1, -1):
                nc.gpsimd.tensor_tensor(wk_sb[:, k, :], wk_sb[:, 0, :], cw_sb[:, k, :], ALU.mult).then_inc(s["w_scaled"], 1)
            with pool.Fori(0, NB) as b:
                pool.wait_ge(s["xn_w"], b * TT + TT)
                nc.gpsimd.tensor_tensor(acc[:, bass.ds(b * TT, TT), :], x_sb[:, bass.ds(b * TT, TT), :], xn_st[:, :, :],
                                        ALU.add).then_inc(s["acc_w"], 1)

            def step(b, q, k, more, back):
                n = b * S + k
                wait(pool, "dbu_rdy", 2 * (n - 1))
                if k == 0:
                    pool.wait_ge(s["dut_rdy"], 2 * b + 2)
                pool.sem_inc(s["pool_go"], 1)
                for t in range(TT):
                    last = nc.gpsimd.tensor_scalar(dbuT[k % 2][:, t, :], duT[q][:, t, :], bc_sb[q][:, t, k:k + 1], 1.0,
                                                   ALU.mult, ALU.mult)
                last.then_inc(s["dbuT_rdy"], 1)
                if back and k == 3:
                    gate(b - 1, 1 - q)
                if more:
                    front(b + 1, 1 - q, k)

            def gate(b, q):
                for hf in range(NH):
                    pool.wait_ge(s["g_sum"], 2 * b + hf + 1)
                    if hf == 0:
                        pool.wait_ge(s["z_rdy"], 2 * b + 2)
                    nc.gpsimd.tensor_tensor(g_sb[:, hf, :], g_sb[:, hf, :], zs_sb[q][:, hf, :], ALU.mult).then_inc(s["g_rdy"], 1)

            def front(b, q, k):
                if k == 6:
                    pool.wait_ge(s["sp_exp"], b + 1)
                    pool.sem_inc(s["pool_go"], 1)
                    nc.gpsimd.tensor_scalar(sp_d[:, :, :], sp_y[:, :, :], 1.0, -1.0, ALU.add, ALU.add).then_inc(s["sp_pool"], 1)
                    pool.wait_ge(s["sp_pool"], 3 * b + 1)
                    pool.wait_ge(s["sp_ln"], b + 1)
                    nc.gpsimd.tensor_tensor(sp_y[:, :, :], sp_y[:, :, :], sp_d[:, :, :], ALU.subtract).then_inc(s["sp_pool"], 1)
                if k == 7:
                    pool.wait_ge(s["sp_pool"], 3 * b + 2)
                    nc.gpsimd.tensor_tensor(sp_l[:, :, :], sp_l[:, :, :], sp_y[:, :, :], ALU.add).then_inc(s["sp_pool"], 1)
                if k == 8:
                    pool.wait_ge(s["sp_pool"], 3 * b + 3)
                    wait(pool, "da_rdy", 2 * S * (b - 1))
                    nc.gpsimd.tensor_tensor(delta[q][:, :, :], sp_l[:, :, :], sp_m[:, :, :], ALU.add).then_inc(s["delta_rdy"], 1)
                if k == 9:
                    pool.wait_ge(s["delta_rdy"], b + 1)
                    wait(pool, "dut_mm", 2 * b)
                    nc.gpsimd.tensor_tensor(du[:, :, :], delta[q][:, :, :], u_sb[q][:, :, :], ALU.mult).then_inc(s["du_rdy"], 1)

            for k in range(S):
                front(0, 0, k)
            for k in range(S):
                step(0, 0, k, True, False)
            with pool.Fori(0, (NB - 2) // 2) as j:
                for k in range(S):
                    step(2 * j + 1, 1, k, True, True)
                for k in range(S):
                    step(2 * j + 2, 0, k, True, True)
            for k in range(S):
                step(NB - 1, 1, k, False, True)
            gate(NB - 1, 1)

        @block.vector
        def _(dve):
            cnt = [0]

            def st(ins):
                cnt[0] += 1
                ins.then_inc(s["st"], 1)
                dve.wait_ge(s["st"], cnt[0])

            dve.wait_ge(s["in_x"], NB * 16)
            with dve.Fori(0, NB) as b:
                for t in range(TT):
                    nc.vector.bn_stats(stat[:, b * TT + t, :], x_sb[:, b * TT + t, :]).then_inc(s["stats_bn"], 1)
            dve.wait_ge(s["stats_bn"], NT)
            me, mo = stat[:, :, 1], stat[:, :, 4]
            var, v1, a, root = tmp[2], tmp[0], tmp[3], tmp[1]

            def inverse_root(dst, roots):
                dve.wait_ge(s["rms_rt"], roots)
                st(nc.vector.reciprocal(dst[:, :], root[:, :]))
                st(nc.vector.tensor_tensor(a[:, :], dst[:, :], dst[:, :], ALU.mult))
                st(nc.vector.tensor_tensor(a[:, :], a[:, :], v1[:, :], ALU.mult))
                st(nc.vector.tensor_scalar(a[:, :], a[:, :], -0.5, 1.5, ALU.mult, ALU.add))
                st(nc.vector.tensor_tensor(dst[:, :], dst[:, :], a[:, :], ALU.mult))

            st(nc.vector.tensor_tensor(mean[:, :], me, mo, ALU.add))
            st(nc.vector.tensor_tensor(a[:, :], me, mo, ALU.subtract))
            st(nc.vector.tensor_tensor(v1[:, :], stat[:, :, 2], stat[:, :, 5], ALU.add))
            st(nc.vector.tensor_scalar(mean[:, :], mean[:, :], 0.5, None, ALU.mult))
            st(nc.vector.scalar_tensor_tensor(a[:, :], a[:, :], 0.25, a[:, :], ALU.mult, ALU.mult))
            st(nc.vector.scalar_tensor_tensor(var[:, :], v1[:, :], 1.0 / H, a[:, :], ALU.mult, ALU.add))
            st(nc.vector.tensor_scalar(v1[:, :], var[:, :], LN_EPS, None, ALU.add))
            assert cnt[0] == ST_LN
            inverse_root(rstd, 1)
            st(nc.vector.tensor_tensor(a[:, :], rstd[:, :], rstd[:, :], ALU.mult))
            st(nc.vector.tensor_tensor(a[:, :], a[:, :], var[:, :], ALU.mult))
            st(nc.vector.tensor_scalar(v1[:, :], a[:, :], RMS_EPS, None, ALU.add))
            assert cnt[0] == ST_RMS
            inverse_root(rms, 2)

            def norm(b):
                wait(dve, "xh_w", TT * b)
                wait(dve, "acc_w", b)
                wait(dve, "xn_pe", b)
                for t in range(TT):
                    i = b * TT + t
                    nc.vector.tensor_scalar(xn_st[:, t, :], x_sb[:, bass.ds(i, 1), :], mean[:, bass.ds(i, 1)],
                                            rstd[:, bass.ds(i, 1)], ALU.subtract, ALU.mult).then_inc(s["xn_w"], 1)
                dve.wait_ge(s["xn_pe"], b + 1)
                nc.vector.tensor_copy(xnT[:, bass.ds(b * T, T)], bank[0][:, :]).then_inc(s["xnT_c"], 1)

            norm(0)
            with dve.Fori(1, NB) as b:
                norm(b)

            dve.wait_ge(s["lgmm"], NT)
            bcast = lambda v: v[:, :].unsqueeze(2).to_broadcast([P, NT, E])
            ranks = rank_sb[:, :].unsqueeze(1).to_broadcast([P, NT, E])
            dve.wait_ge(s["in_small"], SMALL)
            st(nc.vector.tensor_copy(lg[:, :, :].rearrange("p n e -> p (n e)"), bank[2][:, 0:NT * E]))
            for m, oh in ((m1, oh1), (m2, oh2)):
                st(nc.vector.tensor_reduce(m[:, :], lg[:, :, :], AX.X, ALU.max))
                st(nc.vector.tensor_tensor(key[:, :, :], lg[:, :, :], bcast(m), ALU.is_equal))
                st(nc.vector.tensor_tensor(key[:, :, :], key[:, :, :], ranks, ALU.mult))
                st(nc.vector.tensor_reduce(kk[:, :], key[:, :, :], AX.X, ALU.max))
                st(nc.vector.tensor_tensor(oh[:, :, :], bcast(kk), ranks, ALU.is_equal))
                if m is m1:
                    st(nc.vector.scalar_tensor_tensor(lg[:, :, :], oh[:, :, :], -3.0e38, lg[:, :, :], ALU.mult, ALU.add))
            st(nc.vector.tensor_tensor(kk[:, :], m2[:, :], m1[:, :], ALU.subtract))
            assert cnt[0] == ST_TOP
            dve.wait_ge(s["exp_rt"], 1)
            st(nc.vector.tensor_scalar(p1[:, :], p2[:, :], 1.0, None, ALU.add))
            st(nc.vector.reciprocal(p1[:, :], p1[:, :]))
            st(nc.vector.tensor_tensor(p2[:, :], p2[:, :], p1[:, :], ALU.mult))
            st(nc.vector.tensor_tensor(oh1[:, :, :], oh1[:, :, :], bcast(p1), ALU.mult))
            st(nc.vector.tensor_tensor(oh2[:, :, :], oh2[:, :, :], bcast(p2), ALU.mult))
            st(nc.vector.tensor_tensor(gates[:, :, :], oh1[:, :, :], oh2[:, :, :], ALU.add))

            dve.wait_ge(s["acc_w"], NB)

            def experts(b):
                for e in range(E):
                    m = b * E + e
                    for c, (f0, fn) in enumerate(FC):
                        dve.wait_ge(s["sg_rdy"], 3 * m + c + 1)
                        dve.wait_ge(s["u_mm"], 3 * m + c + 1)
                        if c == 0:
                            wait(dve, "y_mm", m)
                        nc.vector.tensor_tensor(hT[0:fn, c, :], sg[0:fn, c, :], bank[3 + c][0:fn, :],
                                                ALU.mult).then_inc(s["ht_w"], 1)
                    dve.wait_ge(s["y_mm"], m + 1)
                    wait(dve, "ep_acc", m * TT)
                    for t in range(TT):
                        i = b * TT + t
                        nc.vector.scalar_tensor_tensor(acc[:, bass.ds(i, 1), :], bank[6][:, t * H:(t + 1) * H],
                                                       gates[:, bass.ds(i, 1), e], acc[:, bass.ds(i, 1), :],
                                                       ALU.mult, ALU.add).then_inc(s["ep_acc"], 1)

            experts(0)
            with dve.Fori(1, NB) as b:
                experts(b)

            def scans(b, k):
                n = b * S + k
                for hf in range(NH):
                    dve.wait_ge(s["da_rdy"], 2 * n + hf + 1)
                    dve.wait_ge(s["dbu_rdy"], 2 * n + hf + 1)
                    if hf == 0:
                        wait(dve, "ht_rdy", 2 * (n - 1))
                    nc.vector.tensor_tensor_scan(h_sb[k % 2][:, hf, :], da[k % 2][:, hf, :], DBU[hf][:, :], 0.0,
                                                 ALU.mult, ALU.add).then_inc(s["h_rdy"], 1)

            def sums(b, q, k):
                n = b * S + k
                for t in range(TT):
                    if t % 2 == 0:
                        dve.wait_ge(s["ht_rdy"], 2 * n + t // 2 + 1)
                    ct = bc_sb[q][:, t, S + k:S + k + 1]
                    if k == 0:
                        if t == 0:
                            wait(dve, "yb_mm", 2 * b)
                        nc.vector.tensor_scalar(y_sb[:, t, :], HT[t // 2][:, t % 2, :], ct, None,
                                                ALU.mult).then_inc(s["y_acc"], 1)
                    else:
                        dve.wait_ge(s["y_acc"], TT * (n - 1) + t + 1)
                        nc.vector.scalar_tensor_tensor(y_sb[:, t, :], HT[t // 2][:, t % 2, :], ct, y_sb[:, t, :],
                                                       ALU.mult, ALU.add).then_inc(s["y_acc"], 1)

            def skip(b, q):
                wait(dve, "o_mm", b)
                for hf in range(NH):
                    dve.wait_ge(s["yb_mm"], 2 * b + hf + 1)
                    nc.vector.scalar_tensor_tensor(g_sb[:, hf, :], u_sb[q][:, hf, :], d_sb[:, hf:hf + 1], FB[hf][:, :],
                                                   ALU.mult, ALU.add).then_inc(s["g_sum"], 1)

            def store(b):
                dve.wait_ge(s["o_mm"], b + 1)
                a_b = acc[:, bass.ds(b * TT, TT), :]
                nc.vector.tensor_tensor(a_b, FB[0][:, :].rearrange("p (t c) -> p t c", t=TT), a_b,
                                        ALU.add).then_inc(s["o_rdy"], 1)

            def step(b, q, k, back):
                if back and k == 2:
                    skip(b - 1, 1 - q)
                scans(b, k)
                if k > 0:
                    sums(b, q, k - 1)
                elif back:
                    sums(b - 1, 1 - q, S - 1)
                if back and k == 10:
                    store(b - 1)

            dve.wait_ge(s["ep_acc"], NB * E * TT)
            for k in range(S):
                step(0, 0, k, False)
            with dve.Fori(0, (NB - 2) // 2) as j:
                for k in range(S):
                    step(2 * j + 1, 1, k, True)
                for k in range(S):
                    step(2 * j + 2, 0, k, True)
            for k in range(S):
                step(NB - 1, 1, k, True)
            sums(NB - 1, 1, S - 1)
            skip(NB - 1, 1)
            store(NB - 1)

        @block.tensor
        def _(pe):
            MM = nc.tensor.matmul
            pe.wait_ge(s["in_small"], SMALL)

            def turn(b):
                for t in range(TT):
                    pe.wait_ge(s["xn_w"], b * TT + t + 1)
                    if t == 0:
                        wait(pe, "xnT_a", b)
                    last = nc.tensor.transpose(bank[0][:, t * P:(t + 1) * P], xn_st[:, t, :], id_sb[:, :])
                last.then_inc(s["xn_pe"], 1)
                for t in range(TT):
                    pe.wait_ge(s["xh_w"], b * TT + t + 1)
                    if t == 0:
                        wait(pe, "xhT_c", b)
                    last = nc.tensor.transpose(bank[1][:, t * P:(t + 1) * P], xh_st[:, t, :], id_sb[:, :])
                last.then_inc(s["xh_pe"], 1)
                pe.wait_ge(s["xnT_a"], b + 1)
                for t in range(TT):
                    MM(bank[2][:, bass.ds((b * TT + t) * E, E)], xnT_st[:, t * P:(t + 1) * P], wr_sb[:, :],
                       start=True, stop=True).then_inc(s["lgmm"], 1)

            turn(0)
            with pe.Fori(1, NB) as b:
                turn(b)

            pe.wait_ge(s["in_moe"], 16 * 5)
            pe.wait_ge(s["xhT_c"], NB)
            pe.wait_ge(s["st"], ST_TOP)

            def experts(b):
                for e in range(E):
                    m = b * E + e
                    for c, (f0, fn) in enumerate(FC):
                        rhs = xnT[:, bass.ds(b * T, T)]
                        wait(pe, "ht_w", 3 * (m - 1) + c + 1)
                        MM(bank[c][0:fn, :], wg_sb[:, e, f0:f0 + fn], rhs, start=True, stop=True).then_inc(s["g_mm"], 1)
                        MM(bank[3 + c][0:fn, :], wu_sb[:, e, f0:f0 + fn], rhs, start=True, stop=True).then_inc(s["u_mm"], 1)
                    pe.wait_ge(s["ht_w"], 3 * m + 3)
                    wait(pe, "ep_acc", m * TT)
                    for t in range(TT):
                        for c, (f0, fn) in enumerate(FC):
                            last = MM(bank[6][:, t * H:(t + 1) * H], hT[0:fn, c, t * P:(t + 1) * P], wd_sb[0:fn, e, c, :],
                                      start=(c == 0), stop=(c == 2))
                    last.then_inc(s["y_mm"], 1)

            experts(0)
            with pe.Fori(1, NB) as b:
                experts(b)

            def dbu_turn(b, k):
                n = b * S + k
                pe.wait_ge(s["dbuT_rdy"], n + 1)
                for hf in range(NH):
                    wait(pe, "h_rdy", 2 * (n - 1) + hf + 1)
                    for t in range(TT):
                        last = nc.tensor.transpose(DBU[hf][:, t * P:(t + 1) * P], dbuT[k % 2][:, t, hf * P:(hf + 1) * P], id_sb[:, :])
                    last.then_inc(s["dbu_rdy"], 1)

            def h_turn(b, k):
                n = b * S + k
                pe.wait_ge(s["h_rdy"], 2 * n + 2)
                for i in range(2):
                    wait(pe, "y_acc", TT * (n - 1) + 2 * i + 2)
                    for t in (2 * i, 2 * i + 1):
                        for hf in range(NH):
                            last = nc.tensor.transpose(HT[i][:, t % 2, hf * P:(hf + 1) * P], h_sb[k % 2][:, hf, t * P:(t + 1) * P], id_sb[:, :])
                    last.then_inc(s["ht_rdy"], 1)

            def front(b, q, k):
                if k in (2, 3):
                    hf = k - 2
                    if not isinstance(b, int) or b > 1:
                        pe.wait_ge(s["g_sum"], 2 * (b - 2) + hf + 1)
                    for tap in range(K):
                        last = MM(FB[hf][:, :], wk_sb[:, tap, hf * P:(hf + 1) * P], xhT[:, bass.ds(b, 1), tap:tap + T],
                                  start=(tap == 0), stop=(tap == K - 1))
                    last.then_inc(s["xc_mm"], 1)
                if k == 4:
                    pe.wait_ge(s["u_rdy"], 2 * b + 2)
                    for hf in range(NH):
                        last = MM(FB[0][0:R, :], xp_sb[:, hf, 0:R], u_sb[q][:, hf, :], start=(hf == 0), stop=(hf == 1))
                    last.then_inc(s["dtr_mm"], 1)
                if k in (5, 6):
                    hf = k - 5
                    pe.wait_ge(s["dtr_rdy"], b + 1)
                    MM(FB[1 - hf][:, :], dtw_sb[:, hf * P:(hf + 1) * P], dtr_sb[:, :], start=True, stop=True).then_inc(s["v_mm"], 1)
                if k == 6:
                    pe.wait_ge(s["v_out"], 2 * b + 1)
                    for t in range(TT):
                        for hf in range(NH):
                            last = MM(FB[1][:, t * 2 * S:(t + 1) * 2 * S], u_sb[q][:, hf, t * P:(t + 1) * P], xp_sb[:, hf, R:],
                                      start=(hf == 0), stop=(hf == 1))
                    last.then_inc(s["bc_mm"], 1)
                if k in (7, 8):
                    hf = k - 7
                    if hf == 0:
                        pe.wait_ge(s["v_out"], 2 * b + 2)
                    else:
                        pe.wait_ge(s["bc_rdy"], b + 1)
                    MM(FB[hf][:, :], wz_sb[:, hf * P:(hf + 1) * P], xhT[:, bass.ds(b, 1), K - 1:], start=True,
                       stop=True).then_inc(s["z_mm"], 1)
                if k in (13, 14):
                    i = k - 13
                    pe.wait_ge(s["du_rdy"], b + 1)
                    if i == 0:
                        pe.wait_ge(s["z_rdy"], 2 * b + 2)
                    else:
                        wait(pe, "o_rdy", b - 1)
                    for t in (2 * i, 2 * i + 1):
                        for hf in range(NH):
                            last = nc.tensor.transpose(FB[1 - i][:, (t % 2) * C + hf * P:(t % 2) * C + (hf + 1) * P],
                                                       du[:, hf, t * P:(t + 1) * P], id_sb[:, :])
                    last.then_inc(s["dut_mm"], 1)

            def y_turn(b):
                pe.wait_ge(s["y_acc"], TT * S * (b + 1))
                if not isinstance(b, int) or b < NB - 1:
                    pe.wait_ge(s["dut_rdy"], 2 * b + 4)
                for hf in range(NH):
                    for t in range(TT):
                        last = nc.tensor.transpose(FB[hf][:, t * P:(t + 1) * P], y_sb[:, t, hf * P:(hf + 1) * P], id_sb[:, :])
                    last.then_inc(s["yb_mm"], 1)

            def project(b):
                pe.wait_ge(s["g_rdy"], 2 * b + 2)
                if not isinstance(b, int) or b < NB - 1:
                    pe.wait_ge(s["g_sum"], 2 * b + 2)
                for t in range(TT):
                    for hf in range(NH):
                        last = MM(FB[0][:, t * H:(t + 1) * H], g_sb[:, hf, t * P:(t + 1) * P], wo_sb[:, hf, :],
                                  start=(hf == 0), stop=(hf == 1))
                last.then_inc(s["o_mm"], 1)

            def step(b, q, k, more, back):
                dbu_turn(b, k)
                if back and k == 1:
                    y_turn(b - 1)
                if k > 0:
                    h_turn(b, k - 1)
                elif back:
                    h_turn(b - 1, S - 1)
                if more:
                    front(b + 1, 1 - q, k)
                if back and k == 9:
                    if more:
                        pe.wait_ge(s["z_rdy"], 2 * b + 3)
                    project(b - 1)

            pe.wait_ge(s["w_scaled"], 7)
            pe.wait_ge(s["xhT_c"], NB)
            pe.wait_ge(s["x_pad"], 1)
            for k in range(S):
                front(0, 0, k)
            for k in range(S):
                step(0, 0, k, True, False)
            with pe.Fori(0, (NB - 2) // 2) as j:
                for k in range(S):
                    step(2 * j + 1, 1, k, True, True)
                for k in range(S):
                    step(2 * j + 2, 0, k, True, True)
            for k in range(S):
                step(NB - 1, 1, k, False, True)
            h_turn(NB - 1, S - 1)
            y_turn(NB - 1)
            project(NB - 1)


_IN = ["x", "norm_w", "w_in", "conv_w", "conv_b", "x_proj", "dt_proj", "dt_b", "a_log", "d_par", "w_out",
       "w_router", "w_gate", "w_up", "w_down", "ident", "rank8"]


def kernel(L0_attn_x, L0_attn_norm_w, L0_attn_in_proj_w, L0_attn_conv_w, L0_attn_conv_b, L0_attn_x_proj_w,
           L0_attn_dt_proj_w, L0_attn_dt_proj_b, L0_attn_A_log, L0_attn_D_param, L0_attn_out_proj_w,
           L0_ffn_w_router, L0_ffn_w_gate, L0_ffn_w_up, L0_ffn_w_down):
    import concourse.bacc as bacc
    from concourse.bass_utils import run_bass_kernel_spmd

    def halves(a):
        a = np.asarray(a)
        return a.reshape(2, 128, -1).transpose(1, 0, 2)

    arrays = {
        "x": np.asarray(L0_attn_x).reshape(4096, 128),
        "norm_w": np.asarray(L0_attn_norm_w).reshape(128, 1),
        "w_in": np.asarray(L0_attn_in_proj_w).T,
        "conv_w": np.asarray(L0_attn_conv_w)[:, 0, :].T,
        "conv_b": halves(L0_attn_conv_b)[:, :, 0],
        "x_proj": halves(np.asarray(L0_attn_x_proj_w).T),
        "dt_proj": np.asarray(L0_attn_dt_proj_w).T,
        "dt_b": halves(L0_attn_dt_proj_b)[:, :, 0],
        "a_log": halves(L0_attn_A_log),
        "d_par": halves(L0_attn_D_param)[:, :, 0],
        "w_out": halves(np.asarray(L0_attn_out_proj_w).T),
        "w_router": np.asarray(L0_ffn_w_router).T,
        "w_gate": np.asarray(L0_ffn_w_gate),
        "w_up": np.asarray(L0_ffn_w_up),
        "w_down": np.asarray(L0_ffn_w_down),
        "ident": np.eye(128, dtype=np.float32),
        "rank8": np.tile(8.0 - np.arange(8, dtype=np.float32), (128, 1)),
    }
    nc = bacc.Bacc("TRN2", target_bir_lowering=False, num_devices=1)
    sent, args = {}, []
    for name in _IN:
        a = np.ascontiguousarray(arrays[name])
        sent[f"in_{name}"] = a
        args.append(nc.dram_tensor(f"in_{name}", a.shape, mybir.dt.from_np(a.dtype), kind="ExternalInput").ap())
    out = nc.dram_tensor("out", (4096, 128), FP32, kind="ExternalOutput").ap()
    build(nc, *args, out)
    r = run_bass_kernel_spmd(nc, [sent], core_ids=[0])
    return r.results[0]["out"].reshape(8, 512, 128)
```

```python
import numpy as np
import concourse.bass as bass
from concourse import mybir
from contextlib import ExitStack

FP32 = mybir.dt.float32
ALU = mybir.AluOpType
ACT = mybir.ActivationFunctionType
AX = mybir.AxisListType


def build(nc, x, norm_w, w_in, conv_w, conv_b, x_proj, dt_proj, dt_b, a_log, d_par, w_out,
          w_router, w_gate, w_up, w_down, ident, rank8, before, steps, x_slots, y_slots, out):
    P = 128
    NB, T, H = 8, 512, 128
    TT = T // P
    NT = NB * TT
    NH = 2
    C = NH * P
    S = 16
    K = conv_w.shape[0]
    R = dt_proj.shape[0]
    E, F = w_gate.shape[0], w_gate.shape[2]
    FC = [(f, min(128, F - f)) for f in range(0, F, 128)]
    NJ = 72
    assert NJ * P >= 2 * NT * P + E * (P - 1) and x_slots.shape[0] == NJ * P
    MB = NJ // (NB - 2)
    NG = 4
    LN_EPS = 1e-5
    RMS_EPS = float(np.finfo(np.float32).eps)
    ST_LN, ST_RMS, ST_NORM, ST_TOP, ST_SEL, ST_SLOT, ST_TILE = 7, 15, 20, 33, 34, 55, 59

    ctx = ExitStack()
    with ctx:
        def sb(name, shape, dt=FP32):
            return ctx.enter_context(nc.sbuf_tensor(name, shape, dt))

        def sem(name):
            return ctx.enter_context(nc.semaphore(name))

        id_sb = sb("id_sb", [P, P])
        rank_sb = sb("rank_sb", [P, E])
        nw_sb = sb("nw_sb", [P, 1])
        wk_sb = sb("wk_sb", [P, K, C])
        wz_sb = sb("wz_sb", [P, C])
        cb_sb = sb("cb_sb", [P, NH])
        xp_sb = sb("xp_sb", [P, NH, R + 2 * S])
        dtw_sb = sb("dtw_sb", [R, C])
        dtb_sb = sb("dtb_sb", [P, NH])
        a_sb = sb("a_sb", [P, NH, S])
        d_sb = sb("d_sb", [P, NH])
        wo_sb = sb("wo_sb", [P, NH, H])
        wr_sb = sb("wr_sb", [P, E])
        wg_sb = sb("wg_sb", [P, E, F])
        wu_sb = sb("wu_sb", [P, E, F])
        wd_sb = sb("wd_sb", [P, E, 3, H])

        x_sb = sb("x_sb", [P, NT, H])
        stat = sb("stat", [P, NT, 6])
        tmp = [sb(f"tmp{i}", [P, NT]) for i in range(4)]
        mean = sb("mean", [P, NT])
        rstd = sb("rstd", [P, NT])
        rms = sb("rms", [P, NT])
        xn_all = sb("xn_all", [P, NT, H])
        before_sb = sb("before_sb", [P, P])
        ones_sb = sb("ones_sb", [P, P])
        steps_sb = sb("steps_sb", [P, NT + NJ])
        zero_sb = sb("zero_sb", [P, NT])
        xhT = sb("xhT", [P, NB, T + K - 1])

        lg = sb("lg", [P, NT, E])
        oh1 = sb("oh1", [P, NT, E])
        oh2 = sb("oh2", [P, NT, E])
        key = sb("key", [P, NT, E])
        m1 = sb("m1", [P, NT])
        m2 = sb("m2", [P, NT])
        kk = sb("kk", [P, NT])
        p1 = sb("p1", [P, NT])
        p2 = sb("p2", [P, NT])
        sel = sb("sel", [P, NT, E])
        rank = sb("rank", [P, NT, E])
        tot = sb("tot", [P, NT, E])
        incl = sb("incl", [P, NT, E])
        tiles = sb("tiles", [P, E])
        ends = sb("ends", [P, E])
        base = sb("base", [P, E])
        slot = sb("slot", [P, 2, NT], mybir.dt.int32)
        tkey = sb("tkey", [1, NJ, E])
        tsum = sb("tsum", [1, NJ])
        texp = sb("texp", [1, NJ], mybir.dt.int32)

        acc = x_sb
        xs = [sb(f"xs{i}", [P, H]) for i in range(2)]
        xT = sb("xT", [P, P])
        th = sb("th", [P, F])
        ga = sb("ga", [P, F])
        hid = sb("hid", [P, F])
        hidT = sb("hidT", [P, len(FC), P])
        ys = [sb(f"ys{i}", [P, H]) for i in range(2)]
        yg = sb("yg", [P, NG, 2, H])

        u_sb = [sb(f"u_sb{i}", [P, NH, T]) for i in range(2)]
        zs_sb = [sb(f"zs_sb{i}", [P, NH, T]) for i in range(2)]
        delta = [sb(f"delta{i}", [P, NH, T]) for i in range(2)]
        duT = [sb(f"duT{i}", [P, TT, C]) for i in range(2)]
        bc_sb = [sb(f"bc_sb{i}", [P, TT, 2 * S]) for i in range(2)]
        dtr_sb = sb("dtr_sb", [R, T])
        sp_m = sb("sp_m", [P, NH, T])
        sp_y = sb("sp_y", [P, NH, T])
        sp_l = sb("sp_l", [P, NH, T])
        sp_d = sb("sp_d", [P, NH, T])
        du = sb("du", [P, NH, T])
        dbuT = [sb(f"dbuT{i}", [P, TT, C]) for i in range(2)]
        da = [sb(f"da{i}", [P, NH, T]) for i in range(2)]
        h_sb = [sb(f"h_sb{i}", [P, NH, T]) for i in range(2)]
        y_sb = sb("y_sb", [P, TT, C])
        g_sb = sb("g_sb", [P, NH, T])

        xn_st = h_sb[1][:, 0, :].rearrange("p (t h) -> p t h", h=H)
        xh_st = h_sb[1][:, 1, :].rearrange("p (t h) -> p t h", h=H)
        win_sb = sp_l[:, 0, :]
        xnT_st = sp_l[:, 1, :]
        cw_sb = y_sb[:, :, :]
        assert NH * C == T and K == TT

        bank = [ctx.enter_context(nc.psum_tensor(f"bank{i}", [P, 512], FP32)) for i in range(8)]
        DBU = bank[0:2]
        HT = [bank[2 + q][:, :].rearrange("p (a c) -> p a c", a=2) for q in range(2)]
        FB = bank[4:6]
        GB, UB = bank[6], bank[7]

        names = """in_small in_taps in_x in_moe fill w_scaled ones xn_c rk_mm scat xs_in0 xs_in1 xt_mm xt_rdy th_rdy ga_rdy hid_rdy hq_mm hq_rdy dn_mm ys_rdy ys_out0 ys_out1 gat0 gat1 gat2 gat3 comb dbuT_a g_init sp_corr a_ready stats_bn st rms_rt xn_w xh_w xn_pe xnT_a xnT_c xh_pe xhT_c
                   lgmm lg_c rt exp_rt rt_p x_pad acc_w g_mm u_mm 
                   dbuT_p dbu_rdy da_rdy h_rdy ht_rdy y_acc
                   xc_mm u_rdy dtr_mm dtr_rdy v_mm v_out bc_mm bc_rdy z_mm z_rdy sp_exp sp_ln
                   sp_pool delta_rdy du_rdy dut_mm dut_rdy yb_mm g_sum g_rdy o_mm o_rdy o_out pool_go""".split()
        s = {k: sem(k) for k in names}

        BEGIN = {"o_mm": 1, "hid_rdy": 1, "hq_rdy": 1, "dn_mm": 1, "u_mm": 1, "ga_rdy": 1, "hq_mm": 1, "ys_rdy": 1,
                 "ys_out0": 16, "ys_out1": 16}

        def begin(eng, *mine):
            for name in mine:
                eng.sem_inc(s[name], BEGIN[name])

        def wait(eng, name, val):
            val = val + BEGIN.get(name, 0)
            if isinstance(val, int) and val <= 0:
                return
            eng.wait_ge(s[name], val)

        MOE = [k for k in range(S) if k % 4 != 3]
        assert len(MOE) == MB and MB % 2 == 0

        def tile_of(b, k):
            return (b - 1) * MB + sum(m < k for m in MOE)

        def par_of(k):
            return sum(m < k for m in MOE) % 2

        def half_of(b, k):
            return (b - 1) * (MB // 2) + sum(m < k for m in MOE) // 2

        block = ctx.enter_context(nc.Block())

        x_v = x.rearrange("(n p) h -> p n h", p=P)
        out_v = out.rearrange("(n p) h -> p n h", p=P)
        SMALL = 16 * 14
        zblk = g_sb[:, 0, 0:P]

        @block.sync
        def _(sp):
            begin(sp, "ys_out0", "ys_out1")
            for b in range(NB):
                sp.dma_start(x_sb[:, b * TT:(b + 1) * TT, :], x_v[:, b * TT:(b + 1) * TT, :]).then_inc(s["in_x"], 16)
            sp.wait_ge(s["ones"], 3)
            sp.dma_start(x_slots.rearrange("(p a) h -> p (a h)", p=P).rearrange("p (r c) -> p r c", c=P),
                         zblk[:, :].unsqueeze(1).to_broadcast([P, NJ, P])).then_inc(s["fill"], 16)
            sp.dma_start(wg_sb[:, :, :], w_gate.rearrange("e h f -> h e f")).then_inc(s["in_moe"], 16)
            sp.dma_start(wu_sb[:, :, :], w_up.rearrange("e h f -> h e f")).then_inc(s["in_moe"], 16)
            for c, (f0, fn) in enumerate(FC):
                sp.dma_start(wd_sb[0:fn, :, c, :], w_down[:, f0:f0 + fn, :].rearrange("e f h -> f e h")).then_inc(s["in_moe"], 16)

            def load(j, q):
                wait(sp, "xt_mm", j - 1)
                sp.dma_start(xs[q][:, :], x_slots[bass.ds(j * P, P), :]).then_inc(s[f"xs_in{q}"], 16)

            def store(j, q):
                wait(sp, "ys_rdy", j + 1)
                sp.dma_start(y_slots[bass.ds(j * P, P), :], ys[q][:, :]).then_inc(s[f"ys_out{q}"], 16)

            sp.wait_ge(s["scat"], 16 * 2 * NT)
            load(0, 0)
            load(1, 1)
            store(0, 0)
            with sp.Fori(1, NJ // 2) as i:
                load(2 * i, 0)
                store(2 * i - 1, 1)
                load(2 * i + 1, 1)
                store(2 * i, 0)
            store(NJ - 1, 1)
            for b in range(NB):
                if b < NB - 1:
                    sp.wait_ge(s["comb"], 2 * TT * (b + 1))
                else:
                    sp.wait_ge(s["o_rdy"], NB)
                sp.dma_start(out_v[:, b * TT:(b + 1) * TT, :], acc[:, b * TT:(b + 1) * TT, :]).then_inc(s["o_out"], 16)
            sp.wait_ge(s["o_out"], 16 * NB)

        @block.scalar
        def _(act):
            begin(act, "hq_rdy", "ys_rdy")
            for dst, src in ((id_sb[:, :], ident), (rank_sb[:, :], rank8), (nw_sb[:, :], norm_w), (win_sb[:, :], w_in),
                             (cb_sb[:, :], conv_b), (dtb_sb[:, :], dt_b), (d_sb[:, :], d_par), (dtw_sb[:, :], dt_proj),
                             (wr_sb[:, :], w_router), (xp_sb[:, :, :], x_proj), (wo_sb[:, :, :], w_out),
                             (a_sb[:, :, :], a_log), (before_sb[:, :], before), (steps_sb[:, :], steps)):
                act.dma_start(dst, src).then_inc(s["in_small"], 16)
            act.wait_ge(s["in_small"], SMALL)
            nc.scalar.activation(a_sb[:, :, :], a_sb[:, :, :], ACT.Exp).then_inc(s["a_ready"], 1)
            act.wait_ge(s["st"], ST_LN)
            nc.scalar.activation(tmp[1][:, :], tmp[0][:, :], ACT.Sqrt).then_inc(s["rms_rt"], 1)
            act.wait_ge(s["st"], ST_RMS)
            nc.scalar.activation(tmp[1][:, :], tmp[0][:, :], ACT.Sqrt).then_inc(s["rms_rt"], 1)
            act.wait_ge(s["st"], ST_NORM)

            def rescale(b):
                act.wait_ge(s["xn_w"], b * TT + TT)
                wait(act, "xh_pe", b)
                for t in range(TT):
                    nc.scalar.activation(xh_st[:, t, :], xn_st[:, t, :], ACT.Copy,
                                         scale=rms[:, bass.ds(b * TT + t, 1)]).then_inc(s["xh_w"], 1)
                act.wait_ge(s["xn_pe"], b + 1)
                wait(act, "lgmm", TT * b)
                nc.scalar.activation(xnT_st[:, :], bank[0][:, :], ACT.Copy).then_inc(s["xnT_a"], 1)
                act.wait_ge(s["xh_pe"], b + 1)
                nc.scalar.activation(xhT[:, bass.ds(b, 1), K - 1:], bank[1][:, :], ACT.Copy).then_inc(s["xhT_c"], 1)

            rescale(0)
            with act.Fori(1, NB) as b:
                rescale(b)
            act.wait_ge(s["st"], ST_TOP)
            nc.scalar.activation(p2[:, :], kk[:, :], ACT.Exp).then_inc(s["exp_rt"], 1)

            def step(b, q, k, more, moe, edge):
                n = b * S + k
                if edge:
                    wait(act, "dbu_rdy", 2 * (n - 1))
                    if k == 0:
                        act.wait_ge(s["dut_rdy"], 2 * b + 2)
                    for t in range(TT):
                        last = nc.scalar.activation(dbuT[k % 2][:, t, :], duT[q][:, t, :], ACT.Copy,
                                                    scale=bc_sb[q][:, t, k:k + 1])
                    last.then_inc(s["dbuT_a"], 1)
                for hf in range(NH):
                    wait(act, "h_rdy", 2 * (n - 2) + hf + 1)
                    if k == 0 and hf == 0:
                        act.wait_ge(s["delta_rdy"], b + 1)
                    nc.scalar.activation(da[k % 2][:, hf, :], delta[q][:, hf, :], ACT.Exp,
                                         scale=a_sb[:, hf, k:k + 1]).then_inc(s["da_rdy"], 1)
                if moe:
                    experts(b, k)
                if more:
                    front(b + 1, 1 - q, k)

            def experts(b, k):
                j, here, prev = tile_of(b, k), k in MOE, k - 1 in MOE
                if prev:
                    wait(act, "hq_mm", j)
                    wait(act, "dn_mm", j - 1)
                    nc.scalar.activation(hidT[:, :, :].rearrange("p c t -> p (c t)"), GB[:, 0:len(FC) * P],
                                         ACT.Copy).then_inc(s["hq_rdy"], 1)
                if here:
                    act.wait_ge(s["xt_mm"], j + 1)
                    wait(act, "u_mm", j)
                    nc.scalar.activation(xT[:, :], UB[:, 0:P], ACT.Copy).then_inc(s["xt_rdy"], 1)
                if prev:
                    q = 1 - par_of(k) if here else par_of(k - 1)
                    wait(act, "dn_mm", j)
                    wait(act, f"ys_out{q}", 16 * half_of(b, k - 1))
                    nc.scalar.activation(ys[q][:, :], UB[:, 0:H], ACT.Copy).then_inc(s["ys_rdy"], 1)
                if here:
                    act.wait_ge(s["g_mm"], j + 1)
                    wait(act, "ga_rdy", j)
                    nc.scalar.activation(th[:, :], GB[:, 0:F], ACT.Tanh, scale=0.5).then_inc(s["th_rdy"], 1)

            def front(b, q, k):
                if k == 5:
                    wait(act, "g_sum", 2 * (b - 1))
                    wait(act, "du_rdy", b - 1)
                    for hf in range(NH):
                        act.wait_ge(s["xc_mm"], 2 * b + hf + 1)
                        nc.scalar.activation(u_sb[q][:, hf, :], FB[hf][:, :], ACT.Silu,
                                             bias=cb_sb[:, hf:hf + 1]).then_inc(s["u_rdy"], 1)
                if k == 6:
                    act.wait_ge(s["dtr_mm"], b + 1)
                    nc.scalar.activation(dtr_sb[:, :], FB[0][0:R, :], ACT.Copy).then_inc(s["dtr_rdy"], 1)
                if k in (7, 8):
                    hf = k - 7
                    if hf == 0:
                        wait(act, "delta_rdy", b)
                    act.wait_ge(s["v_mm"], 2 * b + hf + 1)
                    nc.scalar.activation(sp_m[:, hf, :], FB[1 - hf][:, :], ACT.Relu, bias=dtb_sb[:, hf:hf + 1])
                    nc.scalar.activation(sp_y[:, hf, :], FB[1 - hf][:, :], ACT.Abs,
                                         bias=dtb_sb[:, hf:hf + 1]).then_inc(s["v_out"], 1)
                    act.wait_ge(s["v_out"], 2 * b + hf + 1)
                    nc.scalar.activation(sp_y[:, hf, :], sp_y[:, hf, :], ACT.Exp, scale=-1.0).then_inc(s["sp_exp"], 1)
                if k == 9:
                    act.wait_ge(s["bc_mm"], b + 1)
                    nc.scalar.activation(bc_sb[q][:, :, :], FB[1][:, 0:TT * 2 * S].rearrange("p (t c) -> p t c", t=TT),
                                         ACT.Copy).then_inc(s["bc_rdy"], 1)
                    act.wait_ge(s["sp_pool"], 2 * b + 1)
                    nc.scalar.activation(sp_l[:, :, :], sp_d[:, :, :], ACT.Ln).then_inc(s["sp_ln"], 1)
                if k == 11:
                    wait(act, "g_rdy", 2 * (b - 1))
                    for hf in range(NH):
                        act.wait_ge(s["z_mm"], 2 * b + hf + 1)
                        nc.scalar.activation(zs_sb[q][:, hf, :], FB[hf][:, :], ACT.Silu).then_inc(s["z_rdy"], 1)
                if k in (14, 15):
                    i = k - 14
                    act.wait_ge(s["dut_mm"], 2 * b + i + 1)
                    nc.scalar.activation(duT[q][:, 2 * i:2 * i + 2, :], FB[1 - i][:, :].rearrange("p (a c) -> p a c", a=2),
                                         ACT.Copy).then_inc(s["dut_rdy"], 1)

            for k in range(S):
                front(0, 0, k)
            for k in range(S):
                step(0, 0, k, True, False, True)
            with act.Fori(0, (NB - 2) // 2) as j:
                for k in range(S):
                    step(2 * j + 1, 1, k, True, True, False)
                for k in range(S):
                    step(2 * j + 2, 0, k, True, True, False)
            for k in range(S):
                step(NB - 1, 1, k, False, False, True)

        @block.gpsimd
        def _(pool):
            with nc.allow_non_contiguous_dma(reason="taps over all partitions"):
                pool.dma_start(cw_sb[:, :, :].rearrange("p k c -> p (k c)"),
                               conv_w.rearrange("(a k) c -> a (k c)", a=1).to_broadcast([P, K * C])).then_inc(s["in_taps"], 16)
            nc.gpsimd.memset(xhT[:, :, 0:K - 1], 0.0).then_inc(s["x_pad"], 1)
            nc.gpsimd.memset(ones_sb[:, :], 1.0).then_inc(s["ones"], 1)
            nc.gpsimd.memset(zero_sb[:, :], 0.0).then_inc(s["ones"], 1)
            nc.gpsimd.memset(zblk, 0.0).then_inc(s["ones"], 1)
            pool.wait_ge(s["in_small"], SMALL)
            pool.wait_ge(s["in_taps"], 16)
            pool.wait_ge(s["a_ready"], 1)
            nc.gpsimd.tensor_scalar(a_sb[:, :, :], a_sb[:, :, :], -1.0, 1.0, ALU.mult, ALU.mult).then_inc(s["w_scaled"], 1)
            nc.gpsimd.tensor_scalar(wz_sb[:, :], win_sb[:, C:2 * C], nw_sb[:, 0:1], 1.0, ALU.mult, ALU.mult).then_inc(s["w_scaled"], 1)
            nc.gpsimd.tensor_scalar(wk_sb[:, 0, :], win_sb[:, 0:C], nw_sb[:, 0:1], 1.0, ALU.mult, ALU.mult).then_inc(s["w_scaled"], 1)
            pool.wait_ge(s["w_scaled"], 3)
            for k in range(K - 1, -1, -1):
                nc.gpsimd.tensor_tensor(wk_sb[:, k, :], wk_sb[:, 0, :], cw_sb[:, k, :], ALU.mult).then_inc(s["w_scaled"], 1)
            with pool.Fori(0, NB) as b:
                pool.wait_ge(s["xn_w"], b * TT + TT)
                nc.gpsimd.tensor_tensor(acc[:, bass.ds(b * TT, TT), :], x_sb[:, bass.ds(b * TT, TT), :], xn_st[:, :, :],
                                        ALU.add).then_inc(s["acc_w"], 1)
                nc.gpsimd.tensor_copy(xn_all[:, bass.ds(b * TT, TT), :], xn_st[:, :, :]).then_inc(s["xn_c"], 1)

            def step(b, q, k, more, back, edge):
                n = b * S + k
                if not edge:
                    pool.wait_ge(s["dbu_rdy"], 2 * (n - 1))
                    if k == 0:
                        pool.wait_ge(s["dut_rdy"], 2 * b + 2)
                    pool.sem_inc(s["pool_go"], 1)
                    for t in range(TT):
                        last = nc.gpsimd.tensor_scalar(dbuT[k % 2][:, t, :], duT[q][:, t, :], bc_sb[q][:, t, k:k + 1], 1.0,
                                                       ALU.mult, ALU.mult)
                    last.then_inc(s["dbuT_p"], 1)
                if back and k == 3:
                    gate(b - 1, 1 - q)
                if more:
                    front(b + 1, 1 - q, k)

            def gate(b, q):
                for hf in range(NH):
                    pool.wait_ge(s["g_sum"], 2 * b + hf + 1)
                    if hf == 0:
                        pool.wait_ge(s["z_rdy"], 2 * b + 2)
                    nc.gpsimd.tensor_tensor(g_sb[:, hf, :], g_sb[:, hf, :], zs_sb[q][:, hf, :], ALU.mult).then_inc(s["g_rdy"], 1)

            def front(b, q, k):
                if k == 8:
                    pool.wait_ge(s["sp_exp"], 2 * b + 2)
                    pool.sem_inc(s["pool_go"], 1)
                    nc.gpsimd.tensor_scalar(sp_d[:, :, :], sp_y[:, :, :], 1.0, 1.0, ALU.add, ALU.mult).then_inc(s["sp_pool"], 1)
                if k == 9:
                    pool.wait_ge(s["sp_corr"], b + 1)
                    nc.gpsimd.tensor_tensor(sp_m[:, :, :], sp_m[:, :, :], sp_y[:, :, :], ALU.subtract).then_inc(s["sp_pool"], 1)
                if k == 10:
                    pool.wait_ge(s["sp_pool"], 2 * b + 2)
                    pool.wait_ge(s["sp_ln"], b + 1)
                    wait(pool, "da_rdy", 2 * S * (b - 1))
                    nc.gpsimd.tensor_tensor(delta[q][:, :, :], sp_l[:, :, :], sp_m[:, :, :], ALU.add).then_inc(s["delta_rdy"], 1)
                if k == 11:
                    pool.wait_ge(s["delta_rdy"], b + 1)
                    wait(pool, "dut_mm", 2 * b)
                    nc.gpsimd.tensor_tensor(du[:, :, :], delta[q][:, :, :], u_sb[q][:, :, :], ALU.mult).then_inc(s["du_rdy"], 1)

            def scatter(n0, n1):
                for n in range(n0, n1):
                    for c in range(2):
                        nc.gpsimd.indirect_dma_start(x_slots, bass.IndirectOffsetOnAxis(ap=slot[:, c, n:n + 1], axis=0),
                                                     xn_all[:, n, :], None).then_inc(s["scat"], 16)

            def gather(n):
                wait(pool, "comb", 2 * (n - NG + 1))
                for c in range(2):
                    nc.gpsimd.indirect_dma_start(yg[:, n % NG, c, :], None, y_slots,
                                                 bass.IndirectOffsetOnAxis(ap=slot[:, c, n:n + 1], axis=0)).then_inc(s[f"gat{n % NG}"], 16)

            for k in range(S):
                front(0, 0, k)
            pool.wait_ge(s["st"], ST_SLOT)
            pool.wait_ge(s["fill"], 16)
            pool.wait_ge(s["xn_c"], NB)
            scatter(0, 20)
            for k in range(S):
                step(0, 0, k, True, False, True)
            scatter(20, NT)
            with pool.Fori(0, (NB - 2) // 2) as j:
                for k in range(S):
                    step(2 * j + 1, 1, k, True, True, False)
                for k in range(S):
                    step(2 * j + 2, 0, k, True, True, False)
            wait(pool, "ys_out0", 16 * NJ // 2)
            wait(pool, "ys_out1", 16 * NJ // 2)
            for k in range(S):
                step(NB - 1, 1, k, False, True, True)
                gather(2 * k)
                gather(2 * k + 1)
            gate(NB - 1, 1)

        @block.vector
        def _(dve):
            begin(dve, "hid_rdy", "ga_rdy")
            cnt = [0]

            def st(ins):
                cnt[0] += 1
                ins.then_inc(s["st"], 1)
                dve.wait_ge(s["st"], cnt[0])

            dve.wait_ge(s["in_x"], NB * 16)
            with dve.Fori(0, NB) as b:
                for t in range(TT):
                    nc.vector.bn_stats(stat[:, b * TT + t, :], x_sb[:, b * TT + t, :]).then_inc(s["stats_bn"], 1)
            dve.wait_ge(s["stats_bn"], NT)
            me, mo = stat[:, :, 1], stat[:, :, 4]
            var, v1, a, root = tmp[2], tmp[0], tmp[3], tmp[1]

            def inverse_root(dst, roots):
                dve.wait_ge(s["rms_rt"], roots)
                st(nc.vector.reciprocal(dst[:, :], root[:, :]))
                st(nc.vector.tensor_tensor(a[:, :], dst[:, :], dst[:, :], ALU.mult))
                st(nc.vector.tensor_tensor(a[:, :], a[:, :], v1[:, :], ALU.mult))
                st(nc.vector.tensor_scalar(a[:, :], a[:, :], -0.5, 1.5, ALU.mult, ALU.add))
                st(nc.vector.tensor_tensor(dst[:, :], dst[:, :], a[:, :], ALU.mult))

            st(nc.vector.tensor_tensor(mean[:, :], me, mo, ALU.add))
            st(nc.vector.tensor_tensor(a[:, :], me, mo, ALU.subtract))
            st(nc.vector.tensor_tensor(v1[:, :], stat[:, :, 2], stat[:, :, 5], ALU.add))
            st(nc.vector.tensor_scalar(mean[:, :], mean[:, :], 0.5, None, ALU.mult))
            st(nc.vector.scalar_tensor_tensor(a[:, :], a[:, :], 0.25, a[:, :], ALU.mult, ALU.mult))
            st(nc.vector.scalar_tensor_tensor(var[:, :], v1[:, :], 1.0 / H, a[:, :], ALU.mult, ALU.add))
            st(nc.vector.tensor_scalar(v1[:, :], var[:, :], LN_EPS, None, ALU.add))
            assert cnt[0] == ST_LN
            inverse_root(rstd, 1)
            st(nc.vector.tensor_tensor(a[:, :], rstd[:, :], rstd[:, :], ALU.mult))
            st(nc.vector.tensor_tensor(a[:, :], a[:, :], var[:, :], ALU.mult))
            st(nc.vector.tensor_scalar(v1[:, :], a[:, :], RMS_EPS, None, ALU.add))
            assert cnt[0] == ST_RMS
            inverse_root(rms, 2)

            def norm(b):
                wait(dve, "xh_w", TT * b)
                wait(dve, "acc_w", b)
                wait(dve, "xn_c", b)
                wait(dve, "xn_pe", b)
                for t in range(TT):
                    i = b * TT + t
                    nc.vector.tensor_scalar(xn_st[:, t, :], x_sb[:, bass.ds(i, 1), :], mean[:, bass.ds(i, 1)],
                                            rstd[:, bass.ds(i, 1)], ALU.subtract, ALU.mult).then_inc(s["xn_w"], 1)

            norm(0)
            with dve.Fori(1, NB) as b:
                norm(b)

            dve.wait_ge(s["lgmm"], NT)
            bcast = lambda v: v[:, :].unsqueeze(2).to_broadcast([P, NT, E])
            ranks = rank_sb[:, :].unsqueeze(1).to_broadcast([P, NT, E])
            dve.wait_ge(s["in_small"], SMALL)
            st(nc.vector.tensor_copy(lg[:, :, :].rearrange("p n e -> p (n e)"), bank[2][:, 0:NT * E]))
            for m, oh in ((m1, oh1), (m2, oh2)):
                st(nc.vector.tensor_reduce(m[:, :], lg[:, :, :], AX.X, ALU.max))
                st(nc.vector.tensor_tensor(key[:, :, :], lg[:, :, :], bcast(m), ALU.is_equal))
                st(nc.vector.tensor_tensor(key[:, :, :], key[:, :, :], ranks, ALU.mult))
                st(nc.vector.tensor_reduce(kk[:, :], key[:, :, :], AX.X, ALU.max))
                st(nc.vector.tensor_tensor(oh[:, :, :], bcast(kk), ranks, ALU.is_equal))
                if m is m1:
                    st(nc.vector.scalar_tensor_tensor(lg[:, :, :], oh[:, :, :], -3.0e38, lg[:, :, :], ALU.mult, ALU.add))
            st(nc.vector.tensor_tensor(kk[:, :], m2[:, :], m1[:, :], ALU.subtract))
            assert cnt[0] == ST_TOP
            st(nc.vector.tensor_tensor(sel[:, :, :], oh1[:, :, :], oh2[:, :, :], ALU.add))
            assert cnt[0] == ST_SEL
            dve.wait_ge(s["exp_rt"], 1)
            st(nc.vector.tensor_scalar(p1[:, :], p2[:, :], 1.0, None, ALU.add))
            st(nc.vector.reciprocal(p1[:, :], p1[:, :]))
            st(nc.vector.tensor_tensor(p2[:, :], p2[:, :], p1[:, :], ALU.mult))
            st(nc.vector.tensor_scalar(p1[:, :], p1[:, :], 0.5, None, ALU.mult))
            st(nc.vector.tensor_scalar(p2[:, :], p2[:, :], 0.5, None, ALU.mult))

            dve.wait_ge(s["rk_mm"], 2)
            flat = lambda v: v[:, :, :].rearrange("p n e -> p (n e)")
            st(nc.vector.tensor_copy(flat(rank), bank[2][:, 0:NT * E]))
            st(nc.vector.tensor_copy(flat(tot), bank[2][:, NT * E:2 * NT * E]))
            dve.wait_ge(s["ones"], 2)
            for e in range(E):
                last = nc.vector.tensor_tensor_scan(incl[:, :, e], tot[:, :, e], zero_sb[:, :], 0.0, ALU.add, ALU.add)
            st(last)
            st(nc.vector.tensor_tensor(rank[:, :, :], rank[:, :, :], incl[:, :, :], ALU.add))
            st(nc.vector.tensor_tensor(rank[:, :, :], rank[:, :, :], tot[:, :, :], ALU.subtract))
            st(nc.vector.tensor_tensor(key[:, :, :].rearrange("p n e -> p e n"),
                                       incl[:, NT - 1, :].unsqueeze(2).to_broadcast([P, E, NT]),
                                       steps_sb[:, 0:NT].unsqueeze(1).to_broadcast([P, E, NT]), ALU.is_gt))
            st(nc.vector.tensor_reduce(tiles[:, :], key[:, :, :].rearrange("p n e -> p e n"), AX.X, ALU.add))
            st(nc.vector.tensor_tensor_scan(ends[:, :], tiles[:, :], zero_sb[:, 0:E], 0.0, ALU.add, ALU.add))
            st(nc.vector.tensor_tensor(base[:, :], ends[:, :], tiles[:, :], ALU.subtract))
            st(nc.vector.scalar_tensor_tensor(rank[:, :, :], base[:, :].unsqueeze(1).to_broadcast([P, NT, E]), float(P),
                                              rank[:, :, :], ALU.mult, ALU.add))
            for c, oh in enumerate((oh1, oh2)):
                st(nc.vector.tensor_tensor(key[:, :, :], oh[:, :, :], rank[:, :, :], ALU.mult))
                st(nc.vector.tensor_reduce(kk[:, :], key[:, :, :], AX.X, ALU.add))
                st(nc.vector.tensor_copy(slot[:, c, :], kk[:, :]))
            assert cnt[0] == ST_SLOT, cnt
            st(nc.vector.tensor_tensor(tkey[:, :, :], ends[0:1, :].unsqueeze(1).to_broadcast([1, NJ, E]),
                                       steps_sb[0:1, NT:].unsqueeze(2).to_broadcast([1, NJ, E]), ALU.is_le))
            st(nc.vector.tensor_reduce(tsum[:, :], tkey[:, :, :], AX.X, ALU.add))
            st(nc.vector.tensor_scalar(texp[:, :], tsum[:, :], float(E - 1), None, ALU.min))
            st(nc.vector.memset(GB[:, :], 0.0))
            assert cnt[0] == ST_TILE, cnt
            dve.wait_ge(s["acc_w"], NB)

            def scans(b, k):
                n = b * S + k
                for hf in range(NH):
                    dve.wait_ge(s["da_rdy"], 2 * n + hf + 1)
                    dve.wait_ge(s["dbu_rdy"], 2 * n + hf + 1)
                    if hf == 0:
                        wait(dve, "ht_rdy", 2 * (n - 1))
                    nc.vector.tensor_tensor_scan(h_sb[k % 2][:, hf, :], da[k % 2][:, hf, :], DBU[hf][:, :], 0.0,
                                                 ALU.mult, ALU.add).then_inc(s["h_rdy"], 1)

            def sums(b, q, k):
                n = b * S + k
                for t in range(TT):
                    if t % 2 == 0:
                        dve.wait_ge(s["ht_rdy"], 2 * n + t // 2 + 1)
                    ct = bc_sb[q][:, t, S + k:S + k + 1]
                    if k == 0:
                        if t == 0:
                            wait(dve, "yb_mm", 2 * b)
                        nc.vector.tensor_scalar(y_sb[:, t, :], HT[t // 2][:, t % 2, :], ct, None,
                                                ALU.mult).then_inc(s["y_acc"], 1)
                    else:
                        dve.wait_ge(s["y_acc"], TT * (n - 1) + t + 1)
                        nc.vector.scalar_tensor_tensor(y_sb[:, t, :], HT[t // 2][:, t % 2, :], ct, y_sb[:, t, :],
                                                       ALU.mult, ALU.add).then_inc(s["y_acc"], 1)

            def skip(b, q):
                wait(dve, "o_mm", b)
                for hf in range(NH):
                    dve.wait_ge(s["yb_mm"], 2 * b + hf + 1)
                    nc.vector.scalar_tensor_tensor(g_sb[:, hf, :], u_sb[q][:, hf, :], d_sb[:, hf:hf + 1], FB[hf][:, :],
                                                   ALU.mult, ALU.add).then_inc(s["g_sum"], 1)

            def store(b):
                wait(dve, "o_mm", b + 1)
                a_b = acc[:, bass.ds(b * TT, TT), :]
                nc.vector.tensor_tensor(a_b, FB[0][:, :].rearrange("p (t c) -> p t c", t=TT), a_b,
                                        ALU.add).then_inc(s["o_rdy"], 1)

            def experts(b, k):
                j = tile_of(b, k)
                dve.wait_ge(s["th_rdy"], j + 1)
                wait(dve, "hid_rdy", j)
                nc.vector.scalar_tensor_tensor(ga[:, :], th[:, :], 1.0, GB[:, 0:F], ALU.add, ALU.mult).then_inc(s["ga_rdy"], 1)
                wait(dve, "ga_rdy", j + 1)
                wait(dve, "u_mm", j + 1)
                wait(dve, "hq_mm", j)
                nc.vector.tensor_tensor(hid[:, :], ga[:, :], UB[:, 0:F], ALU.mult).then_inc(s["hid_rdy"], 1)

            def combine(n):
                dve.wait_ge(s[f"gat{n % NG}"], 32 * (n // NG + 1))
                if n < NT - TT:
                    dve.wait_ge(s["o_rdy"], n // TT + 1)
                for c, p in enumerate((p1, p2)):
                    if c:
                        dve.wait_ge(s["comb"], 2 * n + 1)
                    nc.vector.scalar_tensor_tensor(acc[:, n, :], yg[:, n % NG, c, :], p[:, n:n + 1], acc[:, n, :],
                                                   ALU.mult, ALU.add).then_inc(s["comb"], 1)

            def step(b, q, k, more, back, moe):
                if back and k == 2:
                    skip(b - 1, 1 - q)
                scans(b, k)
                if k > 0:
                    sums(b, q, k - 1)
                elif back:
                    sums(b - 1, 1 - q, S - 1)
                if moe and k in MOE:
                    experts(b, k)
                if more and k == 9:
                    dve.wait_ge(s["sp_pool"], 2 * b + 3)
                    nc.vector.scalar_tensor_tensor(sp_y[:, :, :], sp_d[:, :, :], -1.0, sp_y[:, :, :], ALU.add,
                                                   ALU.subtract).then_inc(s["sp_corr"], 1)
                if back and k == 13:
                    store(b - 1)
                if not more and k > 0:
                    combine(2 * k - 2)
                    combine(2 * k - 1)

            dve.wait_ge(s["sp_pool"], 1)
            nc.vector.scalar_tensor_tensor(sp_y[:, :, :], sp_d[:, :, :], -1.0, sp_y[:, :, :], ALU.add,
                                           ALU.subtract).then_inc(s["sp_corr"], 1)
            for k in range(S):
                step(0, 0, k, True, False, False)
            with dve.Fori(0, (NB - 2) // 2) as j:
                for k in range(S):
                    step(2 * j + 1, 1, k, True, True, True)
                for k in range(S):
                    step(2 * j + 2, 0, k, True, True, True)
            for k in range(S):
                step(NB - 1, 1, k, False, True, False)
            sums(NB - 1, 1, S - 1)
            combine(NT - 2)
            combine(NT - 1)
            skip(NB - 1, 1)
            dve.wait_ge(s["comb"], 2 * NT)
            store(NB - 1)

        @block.tensor
        def _(pe):
            begin(pe, "o_mm", "dn_mm", "u_mm", "hq_mm")
            MM = nc.tensor.matmul
            pe.wait_ge(s["in_small"], SMALL)

            def turn(b):
                for t in range(TT):
                    pe.wait_ge(s["xn_w"], b * TT + t + 1)
                    if t == 0:
                        wait(pe, "xnT_a", b)
                    last = nc.tensor.transpose(bank[0][:, t * P:(t + 1) * P], xn_st[:, t, :], id_sb[:, :])
                last.then_inc(s["xn_pe"], 1)
                for t in range(TT):
                    pe.wait_ge(s["xh_w"], b * TT + t + 1)
                    if t == 0:
                        wait(pe, "xhT_c", b)
                    last = nc.tensor.transpose(bank[1][:, t * P:(t + 1) * P], xh_st[:, t, :], id_sb[:, :])
                last.then_inc(s["xh_pe"], 1)
                pe.wait_ge(s["xnT_a"], b + 1)
                for t in range(TT):
                    MM(bank[2][:, bass.ds((b * TT + t) * E, E)], xnT_st[:, t * P:(t + 1) * P], wr_sb[:, :],
                       start=True, stop=True).then_inc(s["lgmm"], 1)

            turn(0)
            with pe.Fori(1, NB) as b:
                turn(b)

            def dbu_turn(b, k, edge):
                n = b * S + k
                if edge:
                    pe.wait_ge(s["dbuT_a"], n + 1 if b == 0 else n + 1 - (NB - 2) * S)
                else:
                    pe.wait_ge(s["dbuT_p"], n + 1 - S)
                for hf in range(NH):
                    wait(pe, "h_rdy", 2 * (n - 1) + hf + 1)
                    for t in range(TT):
                        last = nc.tensor.transpose(DBU[hf][:, t * P:(t + 1) * P], dbuT[k % 2][:, t, hf * P:(hf + 1) * P], id_sb[:, :])
                    last.then_inc(s["dbu_rdy"], 1)

            def h_turn(b, k):
                n = b * S + k
                pe.wait_ge(s["h_rdy"], 2 * n + 2)
                for i in range(2):
                    wait(pe, "y_acc", TT * (n - 1) + 2 * i + 2)
                    for t in (2 * i, 2 * i + 1):
                        for hf in range(NH):
                            last = nc.tensor.transpose(HT[i][:, t % 2, hf * P:(hf + 1) * P], h_sb[k % 2][:, hf, t * P:(t + 1) * P], id_sb[:, :])
                    last.then_inc(s["ht_rdy"], 1)

            def front(b, q, k):
                if k in (2, 3, 4, 5):
                    hf, taps = (k - 2) // 2, (0, 1) if k % 2 == 0 else (2, 3)
                    if k % 2 == 0 and (not isinstance(b, int) or b > 1):
                        pe.wait_ge(s["g_sum"], 2 * (b - 2) + hf + 1)
                    for tap in taps:
                        last = MM(FB[hf][:, :], wk_sb[:, tap, hf * P:(hf + 1) * P], xhT[:, bass.ds(b, 1), tap:tap + T],
                                  start=(tap == 0), stop=(tap == K - 1))
                    if k % 2:
                        last.then_inc(s["xc_mm"], 1)
                if k == 6:
                    pe.wait_ge(s["u_rdy"], 2 * b + 2)
                    for hf in range(NH):
                        last = MM(FB[0][0:R, :], xp_sb[:, hf, 0:R], u_sb[q][:, hf, :], start=(hf == 0), stop=(hf == 1))
                    last.then_inc(s["dtr_mm"], 1)
                if k in (7, 8):
                    hf = k - 7
                    pe.wait_ge(s["dtr_rdy"], b + 1)
                    MM(FB[1 - hf][:, :], dtw_sb[:, hf * P:(hf + 1) * P], dtr_sb[:, :], start=True, stop=True).then_inc(s["v_mm"], 1)
                if k == 9:
                    pe.wait_ge(s["v_out"], 2 * b + 1)
                    for t in range(TT):
                        for hf in range(NH):
                            last = MM(FB[1][:, t * 2 * S:(t + 1) * 2 * S], u_sb[q][:, hf, t * P:(t + 1) * P], xp_sb[:, hf, R:],
                                      start=(hf == 0), stop=(hf == 1))
                    last.then_inc(s["bc_mm"], 1)
                if k in (10, 11):
                    hf = k - 10
                    if hf == 0:
                        pe.wait_ge(s["v_out"], 2 * b + 2)
                    else:
                        pe.wait_ge(s["bc_rdy"], b + 1)
                    MM(FB[hf][:, :], wz_sb[:, hf * P:(hf + 1) * P], xhT[:, bass.ds(b, 1), K - 1:], start=True,
                       stop=True).then_inc(s["z_mm"], 1)
                if k in (14, 15):
                    i = k - 14
                    pe.wait_ge(s["du_rdy"], b + 1)
                    if i == 0:
                        pe.wait_ge(s["z_rdy"], 2 * b + 2)
                    else:
                        wait(pe, "o_rdy", b - 1)
                    for t in (2 * i, 2 * i + 1):
                        for hf in range(NH):
                            last = nc.tensor.transpose(FB[1 - i][:, (t % 2) * C + hf * P:(t % 2) * C + (hf + 1) * P],
                                                       du[:, hf, t * P:(t + 1) * P], id_sb[:, :])
                    last.then_inc(s["dut_mm"], 1)

            def y_turn(b):
                pe.wait_ge(s["y_acc"], TT * S * (b + 1))
                if not isinstance(b, int) or b < NB - 1:
                    pe.wait_ge(s["dut_rdy"], 2 * b + 4)
                for hf in range(NH):
                    for t in range(TT):
                        last = nc.tensor.transpose(FB[hf][:, t * P:(t + 1) * P], y_sb[:, t, hf * P:(hf + 1) * P], id_sb[:, :])
                    last.then_inc(s["yb_mm"], 1)

            def project(b):
                pe.wait_ge(s["g_rdy"], 2 * b + 2)
                if not isinstance(b, int) or b < NB - 1:
                    pe.wait_ge(s["g_sum"], 2 * b + 2)
                for t in range(TT):
                    for hf in range(NH):
                        last = MM(FB[0][:, t * H:(t + 1) * H], g_sb[:, hf, t * P:(t + 1) * P], wo_sb[:, hf, :],
                                  start=(hf == 0), stop=(hf == 1))
                last.then_inc(s["o_mm"], 1)

            def hidden_turn(j):
                wait(pe, "hid_rdy", j)
                for c, (f0, fn) in enumerate(FC):
                    last = nc.tensor.transpose(GB[0:fn, c * P:(c + 1) * P], hid[:, f0:f0 + fn], id_sb[:, :])
                last.then_inc(s["hq_mm"], 1)

            def slots_turn(b, k):
                j, q = tile_of(b, k), par_of(k)
                pe.wait_ge(s[f"xs_in{q}"], 16 * (half_of(b, k) + 1))
                wait(pe, "hid_rdy", j)
                if k - 1 not in MOE:
                    wait(pe, "ys_rdy", j)
                nc.tensor.transpose(UB[:, 0:P], xs[q][:, :], id_sb[:, :]).then_inc(s["xt_mm"], 1)

            def expert(j):
                return nc.tensor.value_load(texp[0:1, bass.ds(j, 1)], min_val=0, max_val=E - 1)

            def down(j, e, here):
                wait(pe, "hq_rdy", j)
                if here:
                    pe.wait_ge(s["xt_rdy"], j + 1)
                for c, (f0, fn) in enumerate(FC):
                    last = MM(UB[:, 0:H], hidT[0:fn, c, :], wd_sb[0:fn, bass.ds(e, 1), c, :], start=(c == 0),
                              stop=(c == len(FC) - 1))
                last.then_inc(s["dn_mm"], 1)

            def gate_up(j, e):
                pe.wait_ge(s["xt_rdy"], j + 1)
                wait(pe, "hq_rdy", j)
                MM(GB[:, 0:F], xT[:, :], wg_sb[:, bass.ds(e, 1), :], start=True, stop=True).then_inc(s["g_mm"], 1)
                wait(pe, "ys_rdy", j)
                MM(UB[:, 0:F], xT[:, :], wu_sb[:, bass.ds(e, 1), :], start=True, stop=True).then_inc(s["u_mm"], 1)

            def step(b, q, k, more, back, moe, edge):
                here, prev = moe and k in MOE, moe and k - 1 in MOE
                j = tile_of(b, k)
                dbu_turn(b, k, edge)
                if back and k == 1:
                    y_turn(b - 1)
                if k > 0:
                    h_turn(b, k - 1)
                elif back:
                    h_turn(b - 1, S - 1)
                if prev:
                    hidden_turn(j)
                if here:
                    slots_turn(b, k)
                if more:
                    front(b + 1, 1 - q, k)
                if back and k == 12:
                    if more:
                        pe.wait_ge(s["z_rdy"], 2 * b + 3)
                    project(b - 1)
                if prev:
                    down(j, expert(j - 1), here)
                if here:
                    gate_up(j, expert(j))

            pe.wait_ge(s["w_scaled"], 7)
            pe.wait_ge(s["xhT_c"], NB)
            pe.wait_ge(s["x_pad"], 1)
            for k in range(S):
                front(0, 0, k)
                if k == 5:
                    pe.wait_ge(s["st"], ST_SEL)
                    pe.wait_ge(s["ones"], 1)
                    sel_v = sel[:, :, :].rearrange("p n e -> p (n e)")
                    MM(bank[2][:, 0:NT * E], before_sb[:, :], sel_v, start=True, stop=True).then_inc(s["rk_mm"], 1)
                    MM(bank[2][:, NT * E:2 * NT * E], ones_sb[:, :], sel_v, start=True, stop=True).then_inc(s["rk_mm"], 1)
            pe.wait_ge(s["st"], ST_TILE)
            for k in range(S):
                step(0, 0, k, True, False, False, True)
            pe.wait_ge(s["in_moe"], 16 * (2 + len(FC)))
            with pe.Fori(0, (NB - 2) // 2) as j:
                for k in range(S):
                    step(2 * j + 1, 1, k, True, True, True, False)
                for k in range(S):
                    step(2 * j + 2, 0, k, True, True, True, False)
            for k in range(S):
                step(NB - 1, 1, k, False, True, False, True)
            h_turn(NB - 1, S - 1)
            y_turn(NB - 1)
            project(NB - 1)


_IN = ["x", "norm_w", "w_in", "conv_w", "conv_b", "x_proj", "dt_proj", "dt_b", "a_log", "d_par", "w_out",
       "w_router", "w_gate", "w_up", "w_down", "ident", "rank8", "before", "steps"]


def kernel(L0_attn_x, L0_attn_norm_w, L0_attn_in_proj_w, L0_attn_conv_w, L0_attn_conv_b, L0_attn_x_proj_w,
           L0_attn_dt_proj_w, L0_attn_dt_proj_b, L0_attn_A_log, L0_attn_D_param, L0_attn_out_proj_w,
           L0_ffn_w_router, L0_ffn_w_gate, L0_ffn_w_up, L0_ffn_w_down):
    import concourse.bacc as bacc
    from concourse.bass_utils import run_bass_kernel_spmd

    def halves(a):
        a = np.asarray(a)
        return a.reshape(2, 128, -1).transpose(1, 0, 2)

    arrays = {
        "x": np.asarray(L0_attn_x).reshape(4096, 128),
        "norm_w": np.asarray(L0_attn_norm_w).reshape(128, 1),
        "w_in": np.asarray(L0_attn_in_proj_w).T,
        "conv_w": np.asarray(L0_attn_conv_w)[:, 0, :].T,
        "conv_b": halves(L0_attn_conv_b)[:, :, 0],
        "x_proj": halves(np.asarray(L0_attn_x_proj_w).T),
        "dt_proj": np.asarray(L0_attn_dt_proj_w).T,
        "dt_b": halves(L0_attn_dt_proj_b)[:, :, 0],
        "a_log": halves(L0_attn_A_log),
        "d_par": halves(L0_attn_D_param)[:, :, 0],
        "w_out": halves(np.asarray(L0_attn_out_proj_w).T),
        "w_router": np.asarray(L0_ffn_w_router).T,
        "w_gate": np.asarray(L0_ffn_w_gate),
        "w_up": np.asarray(L0_ffn_w_up),
        "w_down": np.asarray(L0_ffn_w_down),
        "ident": np.eye(128, dtype=np.float32),
        "rank8": np.tile(8.0 - np.arange(8, dtype=np.float32), (128, 1)),
        "before": np.triu(np.ones((128, 128), np.float32), 1),
        "steps": np.tile(np.concatenate([128 * np.arange(32), np.arange(72)]).astype(np.float32), (128, 1)),
    }
    nc = bacc.Bacc("TRN2", target_bir_lowering=False, num_devices=1)
    sent, args = {}, []
    for name in _IN:
        a = np.ascontiguousarray(arrays[name])
        sent[f"in_{name}"] = a
        args.append(nc.dram_tensor(f"in_{name}", a.shape, mybir.dt.from_np(a.dtype), kind="ExternalInput").ap())
    out = nc.dram_tensor("out", (4096, 128), FP32, kind="ExternalOutput").ap()
    x_slots = nc.dram_tensor("x_slots", (72 * 128, 128), FP32, kind="Internal").ap()
    y_slots = nc.dram_tensor("y_slots", (72 * 128, 128), FP32, kind="Internal").ap()
    build(nc, *args, x_slots, y_slots, out)
    r = run_bass_kernel_spmd(nc, [sent], core_ids=[0])
    return r.results[0]["out"].reshape(8, 512, 128)
```

```python
import numpy as np
import concourse.bass as bass
from concourse import mybir
from contextlib import ExitStack

FP32 = mybir.dt.float32
BF16 = mybir.dt.bfloat16
ALU = mybir.AluOpType
ACT = mybir.ActivationFunctionType
AX = mybir.AxisListType


def build(nc, x, norm_w, w_in, conv_w, conv_b, x_proj, x_proj_r, dt_proj, dt_b, a_log, d_par, w_out,
          w_router, w_gate, w_up, w_down, ident, rank8, before, steps, pick, x_slots, y_slots, out):
    P = 128
    NB, T, H = 8, 512, 128
    TT = T // P
    NT = NB * TT
    NH = 2
    C = NH * P
    S = 16
    K = conv_w.shape[0]
    R = dt_proj.shape[0]
    E, F = w_gate.shape[0], w_gate.shape[2]
    FC = [(f, min(128, F - f)) for f in range(0, F, 128)]
    NJ = 72
    assert NJ * P >= 2 * NT * P + E * (P - 1) and x_slots.shape[0] == (NJ + 1) * P
    MB = NJ // (NB - 2)
    KB = 96
    NXS = 4
    ND = 4
    NG = 8
    LN_EPS = 1e-5
    RMS_EPS = float(np.finfo(np.float32).eps)
    ST_LN, ST_RMS, ST_NORM, ST_TOP, ST_SEL, ST_SLOT, ST_TILE = 7, 15, 20, 33, 34, 55, 58

    ctx = ExitStack()
    with ctx:
        def sb(name, shape, dt=FP32):
            return ctx.enter_context(nc.sbuf_tensor(name, shape, dt))

        def sem(name):
            return ctx.enter_context(nc.semaphore(name))

        id_sb = sb("id_sb", [P, P])
        rank_sb = sb("rank_sb", [P, E])
        nw_sb = sb("nw_sb", [P, 1])
        wk_sb = sb("wk_sb", [P, K, C])
        wz_sb = sb("wz_sb", [P, C])
        cb_sb = sb("cb_sb", [P, NH])
        xp_sb = sb("xp_sb", [P, NH, R + 2 * S])
        xr_sb = sb("xr_sb", [R, C])
        wdt_sb = sb("wdt_sb", [P, NH, C])
        dtw_sb = sb("dtw_sb", [R, C])
        dtb_sb = sb("dtb_sb", [P, NH])
        a_sb = sb("a_sb", [P, NH, S])
        d_sb = sb("d_sb", [P, NH])
        wo_sb = sb("wo_sb", [P, NH, H])
        wr_sb = sb("wr_sb", [P, E])
        wg_sb = sb("wg_sb", [P, E, F])
        wu_sb = sb("wu_sb", [P, E, F])
        wd_sb = sb("wd_sb", [P, E, 3, H])

        x_sb = sb("x_sb", [P, NT, H])
        tmp = [sb(f"tmp{i}", [P, NT]) for i in range(4)]
        mean = sb("mean", [P, NT])
        rstd = sb("rstd", [P, NT])
        rms = sb("rms", [P, NT])
        xn_all = sb("xn_all", [P, NT, H])
        steps_sb = sb("steps_sb", [P, NT + NJ])
        zero_sb = sb("zero_sb", [P, NT])
        xhT = sb("xhT", [P, NB, T + K - 1])

        m1 = sb("m1", [P, NT])
        m2 = sb("m2", [P, NT])
        kk = sb("kk", [P, NT])
        p1 = sb("p1", [P, NT])
        p2 = sb("p2", [P, NT])
        sel = sb("sel", [P, NT, E])
        tiles = sb("tiles", [P, E])
        ends = sb("ends", [P, E])
        base = sb("base", [P, E])
        slot = sb("slot", [P, 2, NT], mybir.dt.int32)
        tsum = sb("tsum", [1, NJ])
        texp = sb("texp", [1, NJ], mybir.dt.int32)

        acc = x_sb
        xs = [sb(f"xs{i}", [P, H]) for i in range(NXS)]
        xT = [sb(f"xT{i}", [P, P]) for i in range(2)]
        th = sb("th", [P, F])
        ga = sb("ga", [P, F])
        hid = sb("hid", [P, F])
        hidT = sb("hidT", [P, len(FC), P])
        ys = [sb(f"ys{i}", [P, H]) for i in range(2)]

        u_sb = [sb(f"u_sb{i}", [P, NH, T]) for i in range(2)]
        zs_sb = sb("zs_sb", [P, NH, T])
        delta = [sb(f"delta{i}", [P, NH, T]) for i in range(2)]
        du = [sb(f"du{i}", [P, NH, T]) for i in range(2)]
        b_row = [sb(f"b_row{i}", [KB, T], BF16) for i in range(2)]
        bct_full = sb("bct_full", [P, T])
        bct = bct_full[0:2 * S, :]
        before_sb, ones_sb = bct_full[:, 0:P], bct_full[:, P:2 * P]
        stat = bct_full[:, 2 * P:2 * P + NT * 6].rearrange("p (n s) -> p n s", s=6)
        b_rem = sb("b_rem", [KB, T])
        b_mid = sb("b_mid", [KB, T], BF16)
        b_all = sb("b_all", [P, 2, T])
        pick_sb = sb("pick_sb", [KB, S])
        pick_bf = sb("pick_bf", [KB, S, P], BF16)
        xb_sb = sb("xb_sb", [P, NH, KB])
        bc_sb = [sb(f"bc_sb{i}", [P, TT, 2 * S]) for i in range(2)]
        sp_m = sb("sp_m", [P, NH, T])
        sp_y = sb("sp_y", [P, NH, T])
        sp_l = sb("sp_l", [P, NH, T])
        sp_d = sb("sp_d", [P, NH, T])
        dbu = [sb(f"dbu{i}", [P, NH, T]) for i in range(2)]
        dbuT = [v[:, :, :].rearrange("p h t -> p (h t)").rearrange("p (t c) -> p t c", c=C) for v in dbu]
        duT = b_all[:, :, :].rearrange("p h t -> p (h t)").rearrange("p (t c) -> p t c", c=C)
        da = [sb(f"da{i}", [P, NH, T]) for i in range(ND)]
        h_sb = [sb(f"h_sb{i}", [P, NH, T]) for i in range(2)]
        y_sb = sb("y_sb", [P, TT, C])
        g_sb = sb("g_sb", [P, NH, T])

        xh_st = [v[:, i, :].rearrange("p (t h) -> p t h", h=H) for v in (h_sb[1], da[0], da[1], da[2]) for i in range(2)]
        xnT_st = [da[ND - 1][:, i, :] for i in range(2)]
        win_sb = sp_l[:, 0, :]
        cw_sb = y_sb[:, :, :]
        part_of = lambda v, i: v[:, i // 2, (i % 2) * NT * E:(i % 2 + 1) * NT * E].rearrange("p (n e) -> p n e", e=E)
        lg, oh1, oh2, key = [part_of(h_sb[0], i) for i in range(4)]
        rank, tot, incl = [part_of(g_sb, i) for i in range(1, 4)]
        tkey = delta[1][0:1, :, :].rearrange("p h t -> p (h t)")[:, 0:NJ * E].rearrange("p (j e) -> p j e", e=E)
        yg = [v[:, i // 2, (i % 2) * 2 * H:(i % 2 + 1) * 2 * H].rearrange("p (c h) -> p c h", c=2)
              for v in (sp_y, sp_l) for i in range(4)]
        assert NH * C == T and K == TT

        bank = [ctx.enter_context(nc.psum_tensor(f"bank{i}", [P, 512], FP32)) for i in range(8)]
        DBU = bank[0:2]
        HT = [bank[2 + q][:, :].rearrange("p (a c) -> p a c", a=2) for q in range(2)]
        YB = bank[2:4]
        FB = bank[4:6]
        GB, UB = bank[6], bank[7]
        XB = bank[1]
        XO = len(FC) * P
        TB = (bank[0:2], bank[6:8])

        names = """in_small in_taps in_x0 in_x1 in_x2 in_x3 in_moe fill w_scaled ones rk_mm scat xs_in0 xs_in1
                   xs_in2 xs_in3 xt_mm xt_rdy th_rdy ga_rdy hid_rdy hq_mm hq_rdy dn_mm ys_rdy ys_out0 ys_out1 gat0
                   gat1 gat2 gat3 gat4 gat5 gat6 gat7 comb dbuT_a sp_corr a_ready stats_bn st rms_rt xn_w xh_w
                   xn_pe xnT_a xh_pe xhT_c lgmm exp_rt x_pad acc_w g_mm u_mm bct_rdy bb_mm bb_cp dbu_p pick_rdy
                   pick_dve br_mm br_hi br_rem br_mid br_rdy dbu_rdy da_rdy h_rdy ht_rdy y_acc xc_mm u_rdy v_mm
                   v_out bc_mm bc_rdy z_mm z_rdy sp_exp sp_ln sp_rem sp_w z_th wdt_mm wdt_rdy delta_rdy du_rdy
                   dut_mm dut_rdy yb_mm g_sum g_rdy o_mm o_rdy o_out""".split()
        s = {k: sem(k) for k in names}

        BEGIN = {"o_mm": 1, "hid_rdy": 1, "hq_rdy": 1, "dn_mm": 1, "u_mm": 1, "ga_rdy": 1, "hq_mm": 1, "ys_rdy": 1,
                 "ys_out0": 16, "ys_out1": 16, "xh_pe": 2, "xn_pe": 2, "xnT_a": 2, "xhT_c": 2, "lgmm": 2 * TT, "bb_cp": 2, "dbu_p": 4}

        def begin(eng, *mine):
            for name in mine:
                eng.sem_inc(s[name], BEGIN[name])

        def wait(eng, name, val):
            val = val + BEGIN.get(name, 0)
            if isinstance(val, int) and val <= 0:
                return
            eng.wait_ge(s[name], val)

        MOE = [k for k in range(S) if k % 4 != 3]
        assert len(MOE) == MB and MB % NXS == 0

        def tile_of(b, k):
            return (b - 1) * MB + sum(m < k for m in MOE)

        def par_of(k):
            return sum(m < k for m in MOE) % 2

        def half_of(b, k):
            return (b - 1) * (MB // 2) + sum(m < k for m in MOE) // 2

        MSTEPS = (NB - 2) * S
        Z_STEP = {8: 1, 11: 0}

        block = ctx.enter_context(nc.Block())

        x_v = x.rearrange("(n p) h -> p n h", p=P)
        out_v = out.rearrange("(n p) h -> p n h", p=P)
        SMALL = 16 * 16
        NX, XT = 4, NT // 4
        zblk = g_sb[:, 0, 0:P]

        @block.sync
        def _(sp):
            begin(sp, "ys_out0", "ys_out1")
            for i in range(NX):
                sp.dma_start(x_sb[:, i * XT:(i + 1) * XT, :], x_v[:, i * XT:(i + 1) * XT, :]).then_inc(s[f"in_x{i}"], 16)
            sp.wait_ge(s["ones"], 3)
            sp.wait_ge(s["in_small"], SMALL)
            sp.wait_ge(s[f"in_x{NX - 1}"], 16)
            sp.dma_start(x_slots.rearrange("(p a) h -> p (a h)", p=P).rearrange("p (r c) -> p r c", c=P),
                         zblk[:, :].unsqueeze(1).to_broadcast([P, NJ + 1, P])).then_inc(s["fill"], 16)
            sp.dma_start(wg_sb[:, :, :], w_gate.rearrange("e h f -> h e f")).then_inc(s["in_moe"], 16)
            sp.dma_start(wu_sb[:, :, :], w_up.rearrange("e h f -> h e f")).then_inc(s["in_moe"], 16)
            for c, (f0, fn) in enumerate(FC):
                sp.dma_start(wd_sb[0:fn, :, c, :], w_down[:, f0:f0 + fn, :].rearrange("e f h -> f e h")).then_inc(s["in_moe"], 16)

            def load(j, i):
                wait(sp, "xt_mm", j - NXS + 1)
                sp.dma_start(xs[i][:, :], x_slots[bass.ds(j * P, P), :]).then_inc(s[f"xs_in{i}"], 16)

            def store(j, q):
                wait(sp, "ys_rdy", j + 1)
                sp.dma_start(y_slots[bass.ds(j * P, P), :], ys[q][:, :]).then_inc(s[f"ys_out{q}"], 16)

            sp.wait_ge(s["scat"], 16 * 2 * NT)
            for i in range(NXS):
                load(i, i)
            with sp.Fori(1, NJ // NXS) as n:
                for i in range(NXS):
                    load(NXS * n + i, i)
                    store(NXS * (n - 1) + i, i % 2)
            load(NJ, 0)
            for i in range(NXS):
                store(NJ - NXS + i, i % 2)
            for b in range(NB):
                if b < NB - 1:
                    sp.wait_ge(s["comb"], 2 * TT * (b + 1))
                else:
                    sp.wait_ge(s["o_rdy"], NB)
                sp.dma_start(out_v[:, b * TT:(b + 1) * TT, :], acc[:, b * TT:(b + 1) * TT, :]).then_inc(s["o_out"], 16)
            sp.wait_ge(s["o_out"], 16 * NB)

        def remainder(eng, ops, b, halves=(0, 1)):
            eng.wait_ge(s["sp_corr"], b + 1)
            for hf in halves:
                ops.tensor_tensor(sp_m[:, hf, :], sp_m[:, hf, :], sp_y[:, hf, :], ALU.subtract).then_inc(s["sp_rem"], 1)

        def softplus(eng, ops, b, q, halves=(0, 1)):
            eng.wait_ge(s["sp_ln"], b + 1)
            wait(eng, "da_rdy", 2 * S * (b - 1))
            for hf in halves:
                eng.wait_ge(s["sp_rem"], 2 * b + hf + 1)
                ops.tensor_tensor(delta[q][:, hf, :], sp_l[:, hf, :], sp_m[:, hf, :], ALU.add).then_inc(s["delta_rdy"], 1)

        def input_scale(eng, ops, b, q, halves=(0, 1)):
            if not isinstance(b, int):
                eng.wait_ge(s["dut_mm"], 2)
            for hf in halves:
                eng.wait_ge(s["delta_rdy"], 2 * b + hf + 1)
                ops.tensor_tensor(du[q][:, hf, :], delta[q][:, hf, :], u_sb[q][:, hf, :], ALU.mult).then_inc(s["du_rdy"], 1)

        def gate(eng, ops, b, halves=(0, 1)):
            for hf in halves:
                eng.wait_ge(s["g_sum"], 2 * b + hf + 1)
                if hf == 0:
                    eng.wait_ge(s["z_rdy"], 2 * b + 2)
                ops.tensor_tensor(g_sb[:, hf, :], g_sb[:, hf, :], zs_sb[:, hf, :], ALU.mult).then_inc(s["g_rdy"], 1)

        @block.scalar
        def _(act):
            begin(act, "hq_rdy", "ys_rdy", "xnT_a", "xhT_c", "bb_cp")
            for dst, src in ((id_sb[:, :], ident), (rank_sb[:, :], rank8), (nw_sb[:, :], norm_w), (win_sb[:, :], w_in),
                             (cb_sb[:, :], conv_b), (dtb_sb[:, :], dt_b), (d_sb[:, :], d_par), (dtw_sb[:, :], dt_proj),
                             (wr_sb[:, :], w_router), (xp_sb[:, :, :], x_proj), (xr_sb[:, :], x_proj_r), (wo_sb[:, :, :], w_out),
                             (a_sb[:, :, :], a_log), (before_sb[:, :], before), (steps_sb[:, :], steps), (pick_sb[:, :], pick)):
                act.dma_start(dst, src).then_inc(s["in_small"], 16)
            act.wait_ge(s["in_small"], SMALL)
            nc.scalar.activation(a_sb[:, :, :], a_sb[:, :, :], ACT.Exp).then_inc(s["a_ready"], 1)
            act.wait_ge(s["st"], ST_LN)
            nc.scalar.activation(tmp[1][:, :], tmp[0][:, :], ACT.Sqrt).then_inc(s["rms_rt"], 1)
            act.wait_ge(s["st"], ST_RMS)
            nc.scalar.activation(tmp[1][:, :], tmp[0][:, :], ACT.Sqrt).then_inc(s["rms_rt"], 1)
            def xn_out(b, q):
                wait(act, "xn_pe", b + 1)
                wait(act, "lgmm", TT * (b - 1))
                nc.scalar.activation(xnT_st[q], TB[q][0][:, :], ACT.Copy).then_inc(s["xnT_a"], 1)

            def rescale(b):
                act.wait_ge(s["xn_w"], b * TT + TT)
                for t in range(TT):
                    nc.scalar.activation(xh_st[b][:, t, :], xn_all[:, b * TT + t, :], ACT.Copy,
                                         scale=rms[:, b * TT + t:b * TT + t + 1]).then_inc(s["xh_w"], 1)

            def xh_out(b, q):
                wait(act, "xh_pe", b + 1)
                nc.scalar.activation(xhT[:, bass.ds(b, 1), K - 1:], TB[q][1][:, :], ACT.Copy).then_inc(s["xhT_c"], 1)

            act.wait_ge(s["st"], ST_NORM)
            rescale(0)
            xn_out(0, 0)
            xh_out(0, 0)
            xn_out(1, 1)
            act.wait_ge(s["wdt_mm"], 1)
            nc.scalar.activation(wdt_sb[:, :, :].rearrange("p a c -> p (a c)"), bank[3][:, :], ACT.Copy).then_inc(s["wdt_rdy"], 1)
            rescale(1)
            for b in range(2, NB):
                xn_out(b, b % 2)
                rescale(b)
            act.wait_ge(s["st"], ST_TOP)
            nc.scalar.activation(p2[:, :], kk[:, :], ACT.Exp).then_inc(s["exp_rt"], 1)

            def decay(b, q, k, halves=(0, 1)):
                n = b * S + k
                for hf in halves:
                    wait(act, "h_rdy", 2 * (n - ND) + hf + 1)
                    if k == 0:
                        act.wait_ge(s["delta_rdy"], 2 * b + hf + 1)
                    nc.scalar.activation(da[k % ND][:, hf, :], delta[q][:, hf, :], ACT.Exp,
                                         scale=a_sb[:, hf, k:k + 1]).then_inc(s["da_rdy"], 1)

            def scaled(b, k):
                q = b % 2
                if b == 0:
                    wait(act, "dbu_rdy", 2 * (k - 1))
                    if k == 0:
                        act.wait_ge(s["dut_rdy"], 2)
                elif k < 4:
                    act.wait_ge(s["h_rdy"], 2 * (b * S + k - 1))
                    act.wait_ge(s["dut_rdy"], 4)
                else:
                    act.wait_ge(s["dbu_rdy"], 2 * (S + k - 3))
                for t in range(TT):
                    last = nc.scalar.activation(dbuT[k % 2][:, t, :], duT[:, t, :], ACT.Copy,
                                                scale=bc_sb[q][:, t, k:k + 1])
                last.then_inc(s["dbuT_a"], 1)

            def input_turned(i):
                for c in range(2):
                    act.wait_ge(s["dut_mm"], 2 * i + c + 1)
                    nc.scalar.activation(duT[:, 2 * c:2 * c + 2, :], FB[1 - c][:, :].rearrange("p (a c) -> p a c", a=2),
                                         ACT.Copy).then_inc(s["dut_rdy"], 1)

            def b_copy(b, k):
                m = (b - 1) * S + k
                act.wait_ge(s["bb_mm"], m + 1)
                wait(act, "dbu_p", 2 * (m - 1))
                nc.scalar.activation(b_all[:, k % 2, :], DBU[0][:, :], ACT.Copy).then_inc(s["bb_cp"], 1)

            BEHIND = (3, 4, 5, 6, 7, 11, 12, 13, 15)

            def step(b, q, k, more, moe, edge):
                ahead = (b, q, k + 2) if k + 2 < S else (b + 1, 1 - q, k + 2 - S) if more else None
                here, prev = moe and k in MOE, moe and k - 1 in MOE
                behind = k in BEHIND
                if not edge and not behind:
                    b_copy(ahead[0], ahead[2])
                if here:
                    slots_out(b, k)
                if ahead and not behind:
                    decay(*ahead)
                if edge and k == 0 and not more:
                    wait(act, "dbu_p", 2 * (MSTEPS + 2))
                    input_turned(1)
                if edge and k + 1 < S and (more or k > 0):
                    scaled(b, k + 1)
                if here:
                    gate_out(b, k)
                if prev:
                    hidden_out(b, k)
                if not edge and behind:
                    b_copy(ahead[0], ahead[2])
                if ahead and behind:
                    decay(*ahead)
                if k in Z_STEP:
                    z_gate(b, k)
                if prev:
                    out_out(b, k)
                if more:
                    front(b + 1, 1 - q, k)

            def z_gate(b, k):
                i, hf = int(k > 8), Z_STEP[k]
                if i == 0:
                    wait(act, "g_rdy", 2 * b)
                act.wait_ge(s["z_mm"], 2 * b + i + 1)
                nc.scalar.activation(zs_sb[:, hf, :], FB[hf][:, :], ACT.Tanh, scale=0.5).then_inc(s["z_th"], 1)

            def slots_out(b, k):
                j, q = tile_of(b, k) + 1, 1 - par_of(k)
                act.wait_ge(s["xt_mm"], j + 1)
                nc.scalar.activation(xT[q][:, :], XB[:, XO:XO + P], ACT.Copy).then_inc(s["xt_rdy"], 1)

            def gate_out(b, k):
                j = tile_of(b, k)
                act.wait_ge(s["g_mm"], j + 1)
                wait(act, "ga_rdy", j)
                nc.scalar.activation(th[:, :], GB[:, 0:F], ACT.Tanh, scale=0.5).then_inc(s["th_rdy"], 1)

            def hidden_out(b, k):
                j = tile_of(b, k)
                wait(act, "hq_mm", j)
                wait(act, "dn_mm", j - 1)
                nc.scalar.activation(hidT[:, :, :].rearrange("p c t -> p (c t)"), XB[:, 0:len(FC) * P],
                                     ACT.Copy).then_inc(s["hq_rdy"], 1)

            def out_out(b, k):
                j, q = tile_of(b, k), par_of(k - 1)
                wait(act, "dn_mm", j)
                wait(act, f"ys_out{q}", 16 * half_of(b, k - 1))
                nc.scalar.activation(ys[q][:, :], XB[:, 0:H], ACT.Copy).then_inc(s["ys_rdy"], 1)

            def front(b, q, k):
                if k == 3:
                    wait(act, "g_sum", 2 * (b - 1))
                    wait(act, "du_rdy", 2 * (b - 1))
                    for hf in range(NH):
                        act.wait_ge(s["xc_mm"], 2 * b + hf + 1)
                        nc.scalar.activation(u_sb[q][:, hf, :], FB[hf][:, :], ACT.Silu,
                                             bias=cb_sb[:, hf:hf + 1]).then_inc(s["u_rdy"], 1)
                if k in (5, 6):
                    hf = k - 5
                    if hf == 0:
                        wait(act, "delta_rdy", 2 * b)
                    act.wait_ge(s["v_mm"], 2 * b + hf + 1)
                    nc.scalar.activation(sp_m[:, hf, :], FB[hf][:, :], ACT.Relu, bias=dtb_sb[:, hf:hf + 1])
                    nc.scalar.activation(sp_y[:, hf, :], FB[hf][:, :], ACT.Abs,
                                         bias=dtb_sb[:, hf:hf + 1]).then_inc(s["v_out"], 1)
                    act.wait_ge(s["v_out"], 2 * b + hf + 1)
                    nc.scalar.activation(sp_y[:, hf, :], sp_y[:, hf, :], ACT.Exp, scale=-1.0).then_inc(s["sp_exp"], 1)
                if k == 7:
                    act.wait_ge(s["br_mm"], b + 1)
                    nc.scalar.activation(bct, FB[0][0:2 * S, :], ACT.Copy).then_inc(s["bct_rdy"], 1)
                    if not isinstance(b, int) or b > 0:
                        nc.scalar.activation(b_row[q][:, :], FB[0][0:KB, :], ACT.Copy).then_inc(s["br_hi"], 1)
                if k == 11:
                    act.wait_ge(s["sp_w"], b + 1)
                    nc.scalar.activation(sp_l[:, :, :], sp_d[:, :, :], ACT.Ln).then_inc(s["sp_ln"], 1)
                if k == 9:
                    act.wait_ge(s["bc_mm"], b + 1)
                    nc.scalar.activation(bc_sb[q][:, :, :], FB[0][:, :].rearrange("p (t c) -> p t c", t=TT)[:, :, 0:2 * S],
                                         ACT.Copy).then_inc(s["bc_rdy"], 1)
                    if not isinstance(b, int) or b > 0:
                        act.wait_ge(s["br_rem"], b)
                        nc.scalar.activation(b_row[q][32:64, :], b_rem[32:64, :], ACT.Copy)
                        nc.scalar.activation(b_mid[64:96, :], b_rem[64:96, :], ACT.Copy).then_inc(s["br_mid"], 1)

            for k in range(4):
                front(0, 0, k)
            xh_out(1, 1)
            for k in range(4, 7):
                front(0, 0, k)
            with act.Fori(1, NB // 2) as j:
                xh_out(2 * j, 0)
                xh_out(2 * j + 1, 1)
            front(0, 0, 11)
            for k in range(7, 11):
                front(0, 0, k)
            input_turned(0)
            scaled(0, 0)
            decay(0, 0, 0)
            decay(0, 0, 1)
            for k in range(S):
                step(0, 0, k, True, False, True)
            act.wait_ge(s["xt_mm"], 1)
            nc.scalar.activation(xT[0][:, :], XB[:, XO:XO + P], ACT.Copy).then_inc(s["xt_rdy"], 1)
            b_copy(1, 0)
            b_copy(1, 1)
            with act.Fori(0, (NB - 2) // 2) as j:
                for k in range(S):
                    step(2 * j + 1, 1, k, True, True, False)
                for k in range(S):
                    step(2 * j + 2, 0, k, True, True, False)
            for k in range(S):
                step(NB - 1, 1, k, False, False, True)

        @block.gpsimd
        def _(pool):
            begin(pool, "dbu_p")
            with nc.allow_non_contiguous_dma(reason="taps over all partitions"):
                pool.dma_start(cw_sb[:, :, :].rearrange("p k c -> p (k c)"),
                               conv_w.rearrange("(a k) c -> a (k c)", a=1).to_broadcast([P, K * C])).then_inc(s["in_taps"], 16)
            nc.gpsimd.memset(xhT[:, :, 0:K - 1], 0.0).then_inc(s["x_pad"], 1)
            nc.gpsimd.memset(xb_sb[:, :, :], 0.0).then_inc(s["pick_rdy"], 1)
            nc.gpsimd.memset(bct_full[:, 2 * P + NT * 6:], 0.0).then_inc(s["x_pad"], 1)
            nc.gpsimd.memset(ones_sb[:, :], 1.0).then_inc(s["ones"], 1)
            nc.gpsimd.memset(zero_sb[:, :], 0.0).then_inc(s["ones"], 1)
            nc.gpsimd.memset(zblk, 0.0).then_inc(s["ones"], 1)
            pool.wait_ge(s["in_small"], SMALL)
            pool.wait_ge(s["in_taps"], 16)
            pool.wait_ge(s["a_ready"], 1)
            nc.gpsimd.tensor_scalar(a_sb[:, :, :], a_sb[:, :, :], -1.0, 1.0, ALU.mult, ALU.mult).then_inc(s["w_scaled"], 1)
            nc.gpsimd.tensor_scalar(wz_sb[:, :], win_sb[:, C:2 * C], nw_sb[:, 0:1], 1.0, ALU.mult, ALU.mult).then_inc(s["w_scaled"], 1)
            nc.gpsimd.tensor_scalar(wo_sb[:, :, :], wo_sb[:, :, :], 0.5, 1.0, ALU.mult, ALU.mult).then_inc(s["w_scaled"], 1)
            nc.gpsimd.tensor_scalar(wk_sb[:, 0, :], win_sb[:, 0:C], nw_sb[:, 0:1], 1.0, ALU.mult, ALU.mult).then_inc(s["w_scaled"], 1)
            pool.wait_ge(s["w_scaled"], 4)
            for k in range(K - 1, -1, -1):
                nc.gpsimd.tensor_tensor(wk_sb[:, k, :], wk_sb[:, 0, :], cw_sb[:, k, :], ALU.mult).then_inc(s["w_scaled"], 1)
            pool.wait_ge(s["pick_rdy"], 1)
            for i in range(3):
                n = S if i else 2 * S
                nc.gpsimd.tensor_copy(xb_sb[:, :, i * 32:i * 32 + n], xp_sb[:, :, R:R + n]).then_inc(s["pick_rdy"], 1)
            with pool.Fori(0, NB) as b:
                pool.wait_ge(s["xn_w"], b * TT + TT)
                nc.gpsimd.tensor_tensor(acc[:, bass.ds(b * TT, TT), :], x_sb[:, bass.ds(b * TT, TT), :],
                                        xn_all[:, bass.ds(b * TT, TT), :], ALU.add).then_inc(s["acc_w"], 1)

            def scaled(b, q, k):
                m, n = (b - 1) * S + k, b * S + k
                if k == 0:
                    pool.wait_ge(s["du_rdy"], 2 * b + 2)
                wait(pool, "bb_cp", m + 1)
                pool.wait_ge(s["h_rdy"], 2 * (n - 1))
                for hf in range(NH):
                    nc.gpsimd.tensor_tensor(dbu[k % 2][:, hf, :], du[q][:, hf, :], b_all[:, k % 2, :],
                                            ALU.mult).then_inc(s["dbu_p"], 1)

            def step(b, q, k, more, back, edge):
                if not edge:
                    if k + 1 < S:
                        scaled(b, q, k + 1)
                    else:
                        scaled(b + 1, 1 - q, 0)
                elif not more and k == 0:
                    scaled(b, q, 1)
                if back and more and k in (2, 3):
                    gate(pool, nc.gpsimd, b - 1, (k - 2,))
                if more:
                    front(b + 1, 1 - q, k)

            def front(b, q, k):
                if k in (9, 10):
                    remainder(pool, nc.gpsimd, b, (k - 9,))
                if k in (12, 13):
                    softplus(pool, nc.gpsimd, b, q, (k - 12,))
                if k in (13, 14):
                    input_scale(pool, nc.gpsimd, b, q, (k - 13,))

            def scatter(n0, n1):
                for n in range(n0, n1):
                    for c in range(2):
                        nc.gpsimd.indirect_dma_start(x_slots, bass.IndirectOffsetOnAxis(ap=slot[:, c, n:n + 1], axis=0),
                                                     xn_all[:, n, :], None).then_inc(s["scat"], 16)

            def gather(n):
                last = n - NG
                if last >= 0:
                    pool.wait_ge(s["comb"], 2 * last + (2 if last % 2 else 3))
                for c in range(2):
                    nc.gpsimd.indirect_dma_start(yg[n % NG][:, c, :], None, y_slots,
                                                 bass.IndirectOffsetOnAxis(ap=slot[:, c, n:n + 1], axis=0)).then_inc(s[f"gat{n % NG}"], 16)

            pool.wait_ge(s["st"], ST_SLOT)
            pool.wait_ge(s["fill"], 16)
            scatter(0, NT)
            pool.wait_ge(s["dbu_rdy"], 2 * S)
            scaled(1, 1, 0)
            with pool.Fori(0, (NB - 2) // 2) as j:
                for k in range(S):
                    step(2 * j + 1, 1, k, True, True, False)
                for k in range(S):
                    step(2 * j + 2, 0, k, True, True, False)
            for k in range(S):
                step(NB - 1, 1, k, False, True, True)
                if k == 0:
                    wait(pool, "ys_out0", 16 * NJ // 2)
                    wait(pool, "ys_out1", 16 * NJ // 2)
                    pool.wait_ge(s["delta_rdy"], 2 * NB)
                gather(2 * k)
                gather(2 * k + 1)

        @block.vector
        def _(dve):
            begin(dve, "hid_rdy", "ga_rdy")
            cnt = [0]

            def st(ins):
                cnt[0] += 1
                ins.then_inc(s["st"], 1)
                dve.wait_ge(s["st"], cnt[0])

            for i in range(NX):
                dve.wait_ge(s[f"in_x{i}"], 16)
                for n in range(i * XT, (i + 1) * XT):
                    nc.vector.bn_stats(stat[:, n, :], x_sb[:, n, :]).then_inc(s["stats_bn"], 1)
            dve.wait_ge(s["stats_bn"], NT)
            me, mo = stat[:, :, 1], stat[:, :, 4]
            var, v1, a, root = tmp[2], tmp[0], tmp[3], tmp[1]

            def inverse_root(dst, roots):
                dve.wait_ge(s["rms_rt"], roots)
                st(nc.vector.reciprocal(dst[:, :], root[:, :]))
                st(nc.vector.tensor_tensor(a[:, :], dst[:, :], dst[:, :], ALU.mult))
                st(nc.vector.tensor_tensor(a[:, :], a[:, :], v1[:, :], ALU.mult))
                st(nc.vector.tensor_scalar(a[:, :], a[:, :], -0.5, 1.5, ALU.mult, ALU.add))
                st(nc.vector.tensor_tensor(dst[:, :], dst[:, :], a[:, :], ALU.mult))

            st(nc.vector.tensor_tensor(mean[:, :], me, mo, ALU.add))
            st(nc.vector.tensor_tensor(a[:, :], me, mo, ALU.subtract))
            st(nc.vector.tensor_tensor(v1[:, :], stat[:, :, 2], stat[:, :, 5], ALU.add))
            st(nc.vector.tensor_scalar(mean[:, :], mean[:, :], 0.5, None, ALU.mult))
            st(nc.vector.scalar_tensor_tensor(a[:, :], a[:, :], 0.25, a[:, :], ALU.mult, ALU.mult))
            st(nc.vector.scalar_tensor_tensor(var[:, :], v1[:, :], 1.0 / H, a[:, :], ALU.mult, ALU.add))
            st(nc.vector.tensor_scalar(v1[:, :], var[:, :], LN_EPS, None, ALU.add))
            assert cnt[0] == ST_LN
            inverse_root(rstd, 1)
            st(nc.vector.tensor_tensor(a[:, :], rstd[:, :], rstd[:, :], ALU.mult))
            st(nc.vector.tensor_tensor(a[:, :], a[:, :], var[:, :], ALU.mult))
            st(nc.vector.tensor_scalar(v1[:, :], a[:, :], RMS_EPS, None, ALU.add))
            assert cnt[0] == ST_RMS
            inverse_root(rms, 2)

            with dve.Fori(0, NB) as b:
                for t in range(TT):
                    i = b * TT + t
                    nc.vector.tensor_scalar(xn_all[:, bass.ds(i, 1), :], x_sb[:, bass.ds(i, 1), :], mean[:, bass.ds(i, 1)],
                                            rstd[:, bass.ds(i, 1)], ALU.subtract, ALU.mult).then_inc(s["xn_w"], 1)

            dve.wait_ge(s["in_small"], SMALL)
            nc.vector.tensor_copy(pick_bf[:, :, :], pick_sb[:, :].unsqueeze(2).to_broadcast([KB, S, P])).then_inc(s["pick_dve"], 1)

            wait(dve, "lgmm", NT)
            bcast = lambda v: v[:, :].unsqueeze(2).to_broadcast([P, NT, E])
            ranks = rank_sb[:, :].unsqueeze(1).to_broadcast([P, NT, E])
            dve.wait_ge(s["in_small"], SMALL)
            st(nc.vector.tensor_copy(lg[:, :, :].rearrange("p n e -> p (n e)"), bank[2][:, 0:NT * E]))
            for m, oh in ((m1, oh1), (m2, oh2)):
                st(nc.vector.tensor_reduce(m[:, :], lg[:, :, :], AX.X, ALU.max))
                st(nc.vector.tensor_tensor(key[:, :, :], lg[:, :, :], bcast(m), ALU.is_equal))
                st(nc.vector.tensor_tensor(key[:, :, :], key[:, :, :], ranks, ALU.mult))
                st(nc.vector.tensor_reduce(kk[:, :], key[:, :, :], AX.X, ALU.max))
                st(nc.vector.tensor_tensor(oh[:, :, :], bcast(kk), ranks, ALU.is_equal))
                if m is m1:
                    st(nc.vector.scalar_tensor_tensor(lg[:, :, :], oh[:, :, :], -3.0e38, lg[:, :, :], ALU.mult, ALU.add))
            st(nc.vector.tensor_tensor(kk[:, :], m2[:, :], m1[:, :], ALU.subtract))
            assert cnt[0] == ST_TOP
            st(nc.vector.tensor_tensor(sel[:, :, :], oh1[:, :, :], oh2[:, :, :], ALU.add))
            assert cnt[0] == ST_SEL
            dve.wait_ge(s["exp_rt"], 1)
            st(nc.vector.tensor_scalar(p1[:, :], p2[:, :], 1.0, None, ALU.add))
            st(nc.vector.reciprocal(p1[:, :], p1[:, :]))
            st(nc.vector.tensor_tensor(p2[:, :], p2[:, :], p1[:, :], ALU.mult))
            st(nc.vector.tensor_scalar(p1[:, :], p1[:, :], 0.5, None, ALU.mult))
            st(nc.vector.tensor_scalar(p2[:, :], p2[:, :], 0.5, None, ALU.mult))

            dve.wait_ge(s["rk_mm"], 2)
            flat = lambda v: v[:, :, :].rearrange("p n e -> p (n e)")
            st(nc.vector.tensor_copy(flat(rank), bank[2][:, 0:NT * E]))
            st(nc.vector.tensor_copy(flat(tot), bank[2][:, NT * E:2 * NT * E]))
            dve.wait_ge(s["ones"], 2)
            for e in range(E):
                last = nc.vector.tensor_tensor_scan(incl[:, :, e], tot[:, :, e], zero_sb[:, :], 0.0, ALU.add, ALU.add)
            st(last)
            st(nc.vector.tensor_tensor(rank[:, :, :], rank[:, :, :], incl[:, :, :], ALU.add))
            st(nc.vector.tensor_tensor(rank[:, :, :], rank[:, :, :], tot[:, :, :], ALU.subtract))
            st(nc.vector.tensor_tensor(key[:, :, :].rearrange("p n e -> p e n"),
                                       incl[:, NT - 1, :].unsqueeze(2).to_broadcast([P, E, NT]),
                                       steps_sb[:, 0:NT].unsqueeze(1).to_broadcast([P, E, NT]), ALU.is_gt))
            st(nc.vector.tensor_reduce(tiles[:, :], key[:, :, :].rearrange("p n e -> p e n"), AX.X, ALU.add))
            st(nc.vector.tensor_tensor_scan(ends[:, :], tiles[:, :], zero_sb[:, 0:E], 0.0, ALU.add, ALU.add))
            st(nc.vector.tensor_tensor(base[:, :], ends[:, :], tiles[:, :], ALU.subtract))
            st(nc.vector.scalar_tensor_tensor(rank[:, :, :], base[:, :].unsqueeze(1).to_broadcast([P, NT, E]), float(P),
                                              rank[:, :, :], ALU.mult, ALU.add))
            for c, oh in enumerate((oh1, oh2)):
                st(nc.vector.tensor_tensor(key[:, :, :], oh[:, :, :], rank[:, :, :], ALU.mult))
                st(nc.vector.tensor_reduce(kk[:, :], key[:, :, :], AX.X, ALU.add))
                st(nc.vector.tensor_copy(slot[:, c, :], kk[:, :]))
            assert cnt[0] == ST_SLOT, cnt
            st(nc.vector.tensor_tensor(tkey[:, :, :], ends[0:1, :].unsqueeze(1).to_broadcast([1, NJ, E]),
                                       steps_sb[0:1, NT:].unsqueeze(2).to_broadcast([1, NJ, E]), ALU.is_le))
            st(nc.vector.tensor_reduce(tsum[:, :], tkey[:, :, :], AX.X, ALU.add))
            st(nc.vector.tensor_scalar(texp[:, :], tsum[:, :], float(E - 1), None, ALU.min))
            assert cnt[0] == ST_TILE, cnt
            dve.wait_ge(s["acc_w"], NB)

            def scans(b, k):
                n = b * S + k
                first, last = isinstance(b, int) and b == 0, isinstance(b, int) and b == NB - 1
                for hf in range(NH):
                    dve.wait_ge(s["da_rdy"], 2 * n + hf + 1)
                    if first or last and k > 1:
                        dve.wait_ge(s["dbu_rdy"], 2 * (k if first else S + k - 2) + hf + 1)
                        inp = DBU[hf][:, :]
                    else:
                        wait(dve, "dbu_p", 2 * (n - S) + hf + 1)
                        inp = dbu[k % 2][:, hf, :]
                    if hf == 0:
                        wait(dve, "ht_rdy", 2 * (n - 1))
                    nc.vector.tensor_tensor_scan(h_sb[k % 2][:, hf, :], da[k % ND][:, hf, :], inp, 0.0,
                                                 ALU.mult, ALU.add).then_inc(s["h_rdy"], 1)

            def sums(b, q, k):
                n = b * S + k
                for t in range(TT):
                    if t % 2 == 0:
                        dve.wait_ge(s["ht_rdy"], 2 * n + t // 2 + 1)
                    ct = bc_sb[q][:, t, S + k:S + k + 1]
                    if k == 0:
                        if t == 0:
                            wait(dve, "yb_mm", 2 * b)
                        nc.vector.tensor_scalar(y_sb[:, t, :], HT[t // 2][:, t % 2, :], ct, None,
                                                ALU.mult).then_inc(s["y_acc"], 1)
                    else:
                        dve.wait_ge(s["y_acc"], TT * (n - 1) + t + 1)
                        nc.vector.scalar_tensor_tensor(y_sb[:, t, :], HT[t // 2][:, t % 2, :], ct, y_sb[:, t, :],
                                                       ALU.mult, ALU.add).then_inc(s["y_acc"], 1)

            def skip(b, q):
                wait(dve, "o_mm", b)
                for hf in range(NH):
                    dve.wait_ge(s["yb_mm"], 2 * b + hf + 1)
                    nc.vector.scalar_tensor_tensor(g_sb[:, hf, :], u_sb[q][:, hf, :], d_sb[:, hf:hf + 1], YB[hf][:, :],
                                                   ALU.mult, ALU.add).then_inc(s["g_sum"], 1)

            def store(b):
                wait(dve, "o_mm", b + 1)
                a_b = acc[:, bass.ds(b * TT, TT), :]
                nc.vector.tensor_tensor(a_b, GB[:, :].rearrange("p (t c) -> p t c", t=TT), a_b,
                                        ALU.add).then_inc(s["o_rdy"], 1)

            def experts(b, k):
                j = tile_of(b, k)
                dve.wait_ge(s["th_rdy"], j + 1)
                wait(dve, "hid_rdy", j)
                nc.vector.scalar_tensor_tensor(ga[:, :], th[:, :], 1.0, GB[:, 0:F], ALU.add, ALU.mult).then_inc(s["ga_rdy"], 1)
                wait(dve, "ga_rdy", j + 1)
                wait(dve, "u_mm", j + 1)
                wait(dve, "hq_mm", j)
                nc.vector.tensor_tensor(hid[:, :], ga[:, :], UB[:, 0:F], ALU.mult).then_inc(s["hid_rdy"], 1)

            def combine(n):
                if n < NT - TT:
                    dve.wait_ge(s["o_rdy"], n // TT + 1)
                for c, p in enumerate((p1, p2)):
                    for m in (n, n + 1):
                        if c:
                            dve.wait_ge(s["comb"], 2 * n + 1 + m - n)
                        else:
                            dve.wait_ge(s[f"gat{m % NG}"], 32 * (m // NG + 1))
                        nc.vector.scalar_tensor_tensor(acc[:, m, :], yg[m % NG][:, c, :], p[:, m:m + 1], acc[:, m, :],
                                                       ALU.mult, ALU.add).then_inc(s["comb"], 1)

            def soft(b):
                dve.wait_ge(s["sp_exp"], 2 * b + 2)
                nc.vector.tensor_scalar(sp_d[:, :, :], sp_y[:, :, :], 1.0, None, ALU.add).then_inc(s["sp_w"], 1)
                dve.wait_ge(s["sp_w"], b + 1)
                nc.vector.scalar_tensor_tensor(sp_y[:, :, :], sp_d[:, :, :], -1.0, sp_y[:, :, :], ALU.add,
                                               ALU.subtract).then_inc(s["sp_corr"], 1)

            LATE = (4, 12)

            def step(b, q, k, more, back, moe):
                scans(b, k)
                if moe and k - 1 in LATE:
                    experts(b, k - 1)
                if back and k == 1:
                    skip(b - 1, 1 - q)
                if back and not more and k == 2:
                    gate(dve, nc.vector, b - 1)
                if back and k == (4 if more else 7):
                    store(b - 1)
                if k > 0:
                    sums(b, q, k - 1)
                elif back:
                    sums(b - 1, 1 - q, S - 1)
                if moe and k in MOE and k not in LATE:
                    experts(b, k)
                if more and k == 7:
                    soft(b + 1)
                if k in Z_STEP:
                    z_gate(b, k)
                if more and k in (8, 10):
                    b_rest(b + 1, 1 - q, k)
                if isinstance(b, int) and b == 0:
                    if k == 9:
                        remainder(dve, nc.vector, 1)
                    if k == 12:
                        softplus(dve, nc.vector, 1, 1)
                    if k == 13:
                        input_scale(dve, nc.vector, 1, 1)
                if not more and k > 1:
                    combine(2 * k - 4)

            def b_rest(b, q, k):
                if k == 8:
                    dve.wait_ge(s["br_hi"], b)
                    nc.vector.tensor_tensor(b_rem[:, :], FB[0][0:KB, :], b_row[q][:, :], ALU.subtract).then_inc(s["br_rem"], 1)
                else:
                    dve.wait_ge(s["br_mid"], b)
                    nc.vector.tensor_tensor(b_row[q][64:96, :], b_rem[64:96, :], b_mid[64:96, :],
                                            ALU.subtract).then_inc(s["br_rdy"], 1)

            def z_gate(b, k):
                i, hf = int(k > 8), Z_STEP[k]
                dve.wait_ge(s["z_th"], 2 * b + i + 1)
                nc.vector.scalar_tensor_tensor(zs_sb[:, hf, :], zs_sb[:, hf, :], 1.0, FB[hf][:, :], ALU.add,
                                               ALU.mult).then_inc(s["z_rdy"], 1)

            soft(0)
            remainder(dve, nc.vector, 0)
            softplus(dve, nc.vector, 0, 0)
            input_scale(dve, nc.vector, 0, 0)
            for k in range(S):
                step(0, 0, k, True, False, False)
            with dve.Fori(0, (NB - 2) // 2) as j:
                for k in range(S):
                    step(2 * j + 1, 1, k, True, True, True)
                for k in range(S):
                    step(2 * j + 2, 0, k, True, True, True)
            for k in range(S):
                step(NB - 1, 1, k, False, True, False)
            sums(NB - 1, 1, S - 1)
            skip(NB - 1, 1)
            gate(dve, nc.vector, NB - 1)
            combine(NT - 4)
            combine(NT - 2)
            dve.wait_ge(s["comb"], 2 * NT)
            store(NB - 1)

        @block.tensor
        def _(pe):
            begin(pe, "o_mm", "dn_mm", "u_mm", "hq_mm", "xh_pe", "xn_pe", "lgmm")
            MM = nc.tensor.matmul
            pe.wait_ge(s["in_small"], SMALL)

            def xn_turn(b, q):
                for t in range(TT):
                    pe.wait_ge(s["xn_w"], b * TT + t + 1)
                    if t == 0:
                        wait(pe, "xnT_a", b - 1)
                    last = nc.tensor.transpose(TB[q][0][:, t * P:(t + 1) * P], xn_all[:, b * TT + t, :], id_sb[:, :])
                last.then_inc(s["xn_pe"], 1)

            def logits(b, q):
                wait(pe, "xnT_a", b + 1)
                for t in range(TT):
                    MM(bank[2][:, bass.ds((b * TT + t) * E, E)], xnT_st[q][:, t * P:(t + 1) * P], wr_sb[:, :],
                       start=True, stop=True).then_inc(s["lgmm"], 1)

            def xh_turn(b, q):
                pe.wait_ge(s["xh_w"], b * TT + TT)
                wait(pe, "xhT_c", b - 1)
                for t in range(TT):
                    last = nc.tensor.transpose(TB[q][1][:, t * P:(t + 1) * P], xh_st[b][:, t, :], id_sb[:, :])
                last.then_inc(s["xh_pe"], 1)

            xn_turn(0, 0)
            xh_turn(0, 0)
            xn_turn(1, 1)
            logits(0, 0)
            for hf in range(NH):
                last = MM(bank[3][:, hf * C:(hf + 1) * C], xr_sb[:, hf * P:(hf + 1) * P], dtw_sb[:, :], start=True, stop=True)
            last.then_inc(s["wdt_mm"], 1)
            for b in range(2, NB):
                xn_turn(b, b % 2)
                logits(b - 1, (b - 1) % 2)
            logits(NB - 1, 1)

            def dbu_turn(b, k):
                n = b * S + k
                pe.wait_ge(s["dbuT_a"], k + 1 if b == 0 else S + k - 1)
                if b > 0 and k == 2:
                    wait(pe, "ys_rdy", NJ)
                    wait(pe, "bb_cp", MSTEPS + 2)
                for hf in range(NH):
                    wait(pe, "h_rdy", 2 * (n - 1) + hf + 1)
                    for t in range(TT):
                        last = nc.tensor.transpose(DBU[hf][:, t * P:(t + 1) * P], dbuT[k % 2][:, t, hf * P:(hf + 1) * P], id_sb[:, :])
                    last.then_inc(s["dbu_rdy"], 1)

            def b_spread(b, q, k):
                m = (b - 1) * S + k
                if k == 0:
                    pe.wait_ge(s["br_rdy"], b)
                wait(pe, "bb_cp", m)
                MM(DBU[0][:, :], pick_bf[:, k, :], b_row[q][:, :], start=True, stop=True).then_inc(s["bb_mm"], 1)

            def input_turn(b, q):
                pe.wait_ge(s["du_rdy"], 2 * b + 2)
                pe.wait_ge(s["bc_rdy"], b + 1)
                wait(pe, "z_rdy", 2 * b)
                wait(pe, "br_rem", b)
                for i in range(2):
                    for t in (2 * i, 2 * i + 1):
                        for hf in range(NH):
                            last = nc.tensor.transpose(FB[1 - i][:, (t % 2) * C + hf * P:(t % 2) * C + (hf + 1) * P],
                                                       du[q][:, hf, t * P:(t + 1) * P], id_sb[:, :])
                    last.then_inc(s["dut_mm"], 1)

            def h_turn(b, k, parts=(0, 1)):
                n = b * S + k
                pe.wait_ge(s["h_rdy"], 2 * n + 2)
                if k == 0:
                    wait(pe, "g_sum", 2 * b)
                for i in parts:
                    wait(pe, "y_acc", TT * (n - 1) + 2 * i + 2)
                    for t in (2 * i, 2 * i + 1):
                        for hf in range(NH):
                            last = nc.tensor.transpose(HT[i][:, t % 2, hf * P:(hf + 1) * P], h_sb[k % 2][:, hf, t * P:(t + 1) * P], id_sb[:, :])
                    last.then_inc(s["ht_rdy"], 1)

            TAPS = {0: ((0, 0), (0, 1), (0, 2), (0, 3)), 1: ((1, 0),), 2: ((1, 1), (1, 2), (1, 3))}

            def front(b, q, k):
                for hf, tap in TAPS.get(k, ()):
                    if hf == 0 and tap == 0 and (not isinstance(b, int) or b > 0):
                        if isinstance(b, int):
                            pe.wait_ge(s["dut_rdy"], 2)
                        else:
                            pe.wait_ge(s["z_rdy"], 2 * (b - 1))
                    last = MM(FB[hf][:, :], wk_sb[:, tap, hf * P:(hf + 1) * P], xhT[:, bass.ds(b, 1), tap:tap + T],
                              start=(tap == 0), stop=(tap == K - 1))
                    if tap == K - 1:
                        last.then_inc(s["xc_mm"], 1)
                if k in (4, 5):
                    hf = k - 4
                    if hf == 0:
                        pe.wait_ge(s["u_rdy"], 2 * b + 2)
                        pe.wait_ge(s["wdt_rdy"], 1)
                    for c in range(NH):
                        last = MM(FB[hf][:, :], wdt_sb[:, c, hf * P:(hf + 1) * P], u_sb[q][:, c, :], start=(c == 0), stop=(c == 1))
                    last.then_inc(s["v_mm"], 1)
                if k == 7:
                    pe.wait_ge(s["v_out"], 2 * b + 1)
                    for hf in range(NH):
                        last = MM(FB[0][0:KB, :], xb_sb[:, hf, :], u_sb[q][:, hf, :], start=(hf == 0), stop=(hf == 1))
                    last.then_inc(s["br_mm"], 1)
                if k == 9:
                    pe.wait_ge(s["bct_rdy"], b + 1)
                    if not isinstance(b, int) or b > 0:
                        pe.wait_ge(s["br_rem"], b)
                    for t in range(TT):
                        last = nc.tensor.transpose(FB[0][:, t * P:(t + 1) * P], bct_full[:, t * P:(t + 1) * P], id_sb[:, :])
                    last.then_inc(s["bc_mm"], 1)

            def z_mm(b, k, more):
                hf = Z_STEP[k + 1]
                if more:
                    if hf:
                        pe.wait_ge(s["v_out"], 2 * b + 4)
                    else:
                        pe.wait_ge(s["bc_rdy"], b + 2)
                else:
                    pe.wait_ge(s["dut_rdy"], 4)
                MM(FB[hf][:, :], wz_sb[:, hf * P:(hf + 1) * P], xhT[:, bass.ds(b, 1), K - 1:], start=True,
                   stop=True).then_inc(s["z_mm"], 1)

            def y_turn(b):
                pe.wait_ge(s["y_acc"], TT * S * (b + 1))
                for hf in range(NH):
                    for t in range(TT):
                        last = nc.tensor.transpose(YB[hf][:, t * P:(t + 1) * P], y_sb[:, t, hf * P:(hf + 1) * P], id_sb[:, :])
                    last.then_inc(s["yb_mm"], 1)

            def project(b):
                pe.wait_ge(s["g_rdy"], 2 * b + 2)
                for t in range(TT):
                    for hf in range(NH):
                        last = MM(GB[:, t * H:(t + 1) * H], g_sb[:, hf, t * P:(t + 1) * P], wo_sb[:, hf, :],
                                  start=(hf == 0), stop=(hf == 1))
                last.then_inc(s["o_mm"], 1)

            def hidden_turn(j):
                wait(pe, "hid_rdy", j)
                for c, (f0, fn) in enumerate(FC):
                    last = nc.tensor.transpose(XB[0:fn, c * P:(c + 1) * P], hid[:, f0:f0 + fn], id_sb[:, :])
                last.then_inc(s["hq_mm"], 1)

            def slots_turn(j, i, rounds):
                pe.wait_ge(s[f"xs_in{i}"], 16 * (rounds + 1))
                nc.tensor.transpose(XB[:, XO:XO + P], xs[i][:, :], id_sb[:, :]).then_inc(s["xt_mm"], 1)

            def expert(j):
                return nc.tensor.value_load(texp[0:1, bass.ds(j, 1)], min_val=0, max_val=E - 1)

            def down(j, e):
                wait(pe, "hq_rdy", j)
                for c, (f0, fn) in enumerate(FC):
                    last = MM(XB[:, 0:H], hidT[0:fn, c, :], wd_sb[0:fn, bass.ds(e, 1), c, :], start=(c == 0),
                              stop=(c == len(FC) - 1))
                last.then_inc(s["dn_mm"], 1)

            def gate(j, q, e):
                pe.wait_ge(s["xt_rdy"], j + 1)
                wait(pe, "ga_rdy", j)
                MM(GB[:, 0:F], xT[q][:, :], wg_sb[:, bass.ds(e, 1), :], start=True, stop=True).then_inc(s["g_mm"], 1)

            def up(j, q, e):
                wait(pe, "hid_rdy", j)
                MM(UB[:, 0:F], xT[q][:, :], wu_sb[:, bass.ds(e, 1), :], start=True, stop=True).then_inc(s["u_mm"], 1)

            def step(b, q, k, more, back, moe, edge, e_prev):
                here, prev = moe and k in MOE, moe and k - 1 in MOE
                j = tile_of(b, k)
                e_here = expert(j) if here else None
                h_at = (b, k - 1) if k > 0 else (b - 1, S - 1) if back else None
                if back and k == 1:
                    h_at = None
                if not edge:
                    b_spread(b if k + 2 < S else b + 1, q if k + 2 < S else 1 - q, (k + 2) % S)
                elif back and k == 0:
                    input_turn(b, q)
                elif k > 1 or not back:
                    dbu_turn(b, k)
                if back and k == 1:
                    y_turn(b - 1)
                if h_at:
                    h_turn(*h_at, (0,))
                if here:
                    wait(pe, "ys_rdy", j - 1 if prev else j)
                    pe.wait_ge(s["xt_rdy"], j + 1)
                    i_next = sum(m < k for m in MOE) + 1
                    slots_turn(j + 1, i_next % NXS, (b - 1) * (MB // NXS) + i_next // NXS)
                if h_at:
                    h_turn(*h_at, (1,))
                if here:
                    if k == 4:
                        pe.wait_ge(s["o_rdy"], b)
                    gate(j, par_of(k), e_here)
                if prev:
                    if here:
                        pe.wait_ge(s["xt_rdy"], j + 2)
                    else:
                        wait(pe, "ys_rdy", j - 1)
                    hidden_turn(j)
                if here:
                    up(j, par_of(k), e_here)
                if back and k == 1:
                    h_turn(b, 0)
                if prev and not here:
                    down(j, e_prev)
                if more and k != 4:
                    front(b + 1, 1 - q, k)
                if k + 1 in Z_STEP:
                    z_mm(b, k, more)
                if back and k == (3 if more else 6):
                    project(b - 1)
                if prev and here:
                    down(j, e_prev)
                if more and k == 4:
                    front(b + 1, 1 - q, k)
                return e_here

            def batch(b, q, more, back, moe, edge):
                e = None
                for k in range(S):
                    e = step(b, q, k, more, back, moe, edge, e)

            pe.wait_ge(s["w_scaled"], 8)
            pe.wait_ge(s["x_pad"], 2)
            pe.wait_ge(s["pick_rdy"], 4)
            wait(pe, "xhT_c", 1)
            for k in range(4):
                front(0, 0, k)
            pe.wait_ge(s["st"], ST_SEL)
            pe.wait_ge(s["ones"], 1)
            sel_v = sel[:, :, :].rearrange("p n e -> p (n e)")
            MM(bank[2][:, 0:NT * E], before_sb[:, :], sel_v, start=True, stop=True).then_inc(s["rk_mm"], 1)
            MM(bank[2][:, NT * E:2 * NT * E], ones_sb[:, :], sel_v, start=True, stop=True).then_inc(s["rk_mm"], 1)
            xh_turn(1, 1)
            for k in range(4, 7):
                front(0, 0, k)
            for b in range(2, NB):
                xh_turn(b, b % 2)
            for k in range(7, 11):
                front(0, 0, k)
            wait(pe, "xhT_c", NB)
            input_turn(0, 0)
            pe.wait_ge(s["st"], ST_TILE)
            batch(0, 0, True, False, False, True)
            pe.wait_ge(s["h_rdy"], 2 * S)
            pe.wait_ge(s["pick_dve"], 1)
            slots_turn(0, 0, 0)
            b_spread(1, 1, 0)
            b_spread(1, 1, 1)
            pe.wait_ge(s["in_moe"], 16 * (2 + len(FC)))
            with pe.Fori(0, (NB - 2) // 2) as j:
                batch(2 * j + 1, 1, True, True, True, False)
                batch(2 * j + 2, 0, True, True, True, False)
            batch(NB - 1, 1, False, True, False, True)
            h_turn(NB - 1, S - 1)
            y_turn(NB - 1)
            project(NB - 1)


_IN = ["x", "norm_w", "w_in", "conv_w", "conv_b", "x_proj", "x_proj_r", "dt_proj", "dt_b", "a_log", "d_par", "w_out",
       "w_router", "w_gate", "w_up", "w_down", "ident", "rank8", "before", "steps", "pick"]


def kernel(L0_attn_x, L0_attn_norm_w, L0_attn_in_proj_w, L0_attn_conv_w, L0_attn_conv_b, L0_attn_x_proj_w,
           L0_attn_dt_proj_w, L0_attn_dt_proj_b, L0_attn_A_log, L0_attn_D_param, L0_attn_out_proj_w,
           L0_ffn_w_router, L0_ffn_w_gate, L0_ffn_w_up, L0_ffn_w_down):
    import concourse.bacc as bacc
    from concourse.bass_utils import run_bass_kernel_spmd

    def halves(a):
        a = np.asarray(a)
        return a.reshape(2, 128, -1).transpose(1, 0, 2)

    arrays = {
        "x": np.asarray(L0_attn_x).reshape(4096, 128),
        "norm_w": np.asarray(L0_attn_norm_w).reshape(128, 1),
        "w_in": np.asarray(L0_attn_in_proj_w).T,
        "conv_w": np.asarray(L0_attn_conv_w)[:, 0, :].T,
        "conv_b": halves(L0_attn_conv_b)[:, :, 0],
        "x_proj": halves(np.asarray(L0_attn_x_proj_w).T),
        "x_proj_r": np.asarray(L0_attn_x_proj_w)[:8],
        "dt_proj": np.asarray(L0_attn_dt_proj_w).T,
        "dt_b": halves(L0_attn_dt_proj_b)[:, :, 0],
        "a_log": halves(L0_attn_A_log),
        "d_par": halves(L0_attn_D_param)[:, :, 0],
        "w_out": halves(np.asarray(L0_attn_out_proj_w).T),
        "w_router": np.asarray(L0_ffn_w_router).T,
        "w_gate": np.asarray(L0_ffn_w_gate),
        "w_up": np.asarray(L0_ffn_w_up),
        "w_down": np.asarray(L0_ffn_w_down),
        "ident": np.eye(128, dtype=np.float32),
        "rank8": np.tile(8.0 - np.arange(8, dtype=np.float32), (128, 1)),
        "before": np.triu(np.ones((128, 128), np.float32), 1),
        "steps": np.tile(np.concatenate([128 * np.arange(32), np.arange(72)]).astype(np.float32), (128, 1)),
    }
    arrays["pick"] = np.tile(np.eye(32, 16, dtype=np.float32), (3, 1))
    nc = bacc.Bacc("TRN2", target_bir_lowering=False, num_devices=1)
    sent, args = {}, []
    for name in _IN:
        a = np.ascontiguousarray(arrays[name])
        sent[f"in_{name}"] = a
        args.append(nc.dram_tensor(f"in_{name}", a.shape, mybir.dt.from_np(a.dtype), kind="ExternalInput").ap())
    out = nc.dram_tensor("out", (4096, 128), FP32, kind="ExternalOutput").ap()
    x_slots = nc.dram_tensor("x_slots", (73 * 128, 128), FP32, kind="Internal").ap()
    y_slots = nc.dram_tensor("y_slots", (72 * 128, 128), FP32, kind="Internal").ap()
    build(nc, *args, x_slots, y_slots, out)
    r = run_bass_kernel_spmd(nc, [sent], core_ids=[0])
    return r.results[0]["out"].reshape(8, 512, 128)
```
